# Optimizing a Trainium2 kernel written in Bass

```python
import numpy as np
import jax
import jax.numpy as jnp

def _softmax(x, axis=-1):
    return jax.nn.softmax(x, axis=axis)
def _gelu(x):
    return jax.nn.gelu(x, approximate=True)
def _silu(x):
    return jax.nn.silu(x)
def _sigmoid(x):
    return jax.nn.sigmoid(x)
def _layernorm(x, axis=-1, eps=1e-5):
    m = jnp.mean(x, axis=axis, keepdims=True)
    v = jnp.var(x, axis=axis, keepdims=True)
    return (x - m) / jnp.sqrt(v + eps)
def _scatter_add(tgt, idx, src, axis=0):
    return tgt.at[idx].add(src)
def _segment_sum(src, seg, n):
    return jax.ops.segment_sum(src, seg, n)

kernel_name = 'mk_adj_preln_d2_adj_512_a20f2c'

def setup_inputs(seed: int = 0):
    np.random.seed(seed)
    _w = jnp.asarray
    def _rec_inputs():
        import jax
        import jax.numpy as jnp
        _gk = jax.random.key(seed)
        x = -0.0002928 + 1 * jax.random.normal(jax.random.fold_in(_gk, 1), (4096, 512), jnp.float32)
        _a = jax.random.bernoulli(jax.random.fold_in(_gk, 2), 0.00390625, (4096, 4096))
        _a = jnp.logical_or(_a, jnp.swapaxes(_a, -1, -2))
        _a = jnp.logical_or(_a, jnp.eye(4096, dtype=bool))
        _af = _a.astype(jnp.float32)
        _af = _af * jax.random.uniform(jax.random.fold_in(_gk, 3), (4096, 4096), jnp.float32, 0.05, 1)
        adj = _af
        return x, adj
    x, adj = _rec_inputs()
    def _L0_gnn_setup():
        import jax, jax.numpy as jnp
        import numpy as np
        N = 8192
        D = 512
        key = jax.random.key(seed)
        k_h, k_a, k_q, k_k, k_v = jax.random.split(key, 5)
        H = jax.random.normal(k_h, (N, D), dtype=jnp.float32)
        A = jax.random.uniform(k_a, (N, N), dtype=jnp.float32)
        W_Q = jax.random.uniform(k_q, (D, D), dtype=jnp.float32)
        W_K = jax.random.uniform(k_k, (D, D), dtype=jnp.float32)
        W_V = jax.random.uniform(k_v, (D, D), dtype=jnp.float32)
        return {'H': H, 'A': A, 'W_Q': W_Q, 'W_K': W_K, 'W_V': W_V}
    _L0_gnn_all = _L0_gnn_setup()
    _L0_gnn_in = {k: v for k, v in _L0_gnn_all.items() if k in ('W_Q', 'W_K', 'W_V', )}
    del _L0_gnn_all

    def _L1_gnn_setup():
        import jax, jax.numpy as jnp
        import numpy as np
        N, DIN, F, H = (4096, 512, 64, 8)
        EPS = float(np.finfo(np.float64).eps)
        key = jax.random.key(seed)
        ks = jax.random.split(key, 6)
        scale_k = (6.0 / (DIN + F)) ** 0.5
        scale_a = (6.0 / (F + 1)) ** 0.5
        return {'x': jax.random.normal(ks[0], (N, DIN), jnp.float32), 'adj': jax.random.normal(ks[1], (N, N), jnp.float32), 'kernels': jax.random.uniform(ks[2], (H, DIN, F), jnp.float32, -scale_k, scale_k), 'attn_self': jax.random.uniform(ks[3], (H, F), jnp.float32, -scale_a, scale_a), 'attn_neigh': jax.random.uniform(ks[4], (H, F), jnp.float32, -scale_a, scale_a), 'biases': jnp.zeros((H, F), jnp.float32)}
    _L1_gnn_all = _L1_gnn_setup()
    _L1_gnn_in = {k: v for k, v in _L1_gnn_all.items() if k in ('kernels', 'attn_self', 'attn_neigh', 'biases', )}
    del _L1_gnn_all

    return {
        "x": x,
        "adj": adj,
        "L0_gnn_W_Q": _L0_gnn_in["W_Q"],
        "L0_gnn_W_K": _L0_gnn_in["W_K"],
        "L0_gnn_W_V": _L0_gnn_in["W_V"],
        "L1_gnn_kernels": _L1_gnn_in["kernels"],
        "L1_gnn_attn_self": _L1_gnn_in["attn_self"],
        "L1_gnn_attn_neigh": _L1_gnn_in["attn_neigh"],
        "L1_gnn_biases": _L1_gnn_in["biases"],
    }

def reference(x, adj, L0_gnn_W_Q, L0_gnn_W_K, L0_gnn_W_V, L1_gnn_kernels, L1_gnn_attn_self, L1_gnn_attn_neigh, L1_gnn_biases):
    import jax
    import jax.numpy as jnp
    def _L0_gnn_ref(H, A, W_Q, W_K, W_V):
        import jax, jax.numpy as jnp
        import numpy as np
        N = 8192
        D = 512
        scale = 1.0 / jnp.sqrt(jnp.asarray(H.shape[1], dtype=H.dtype))
        HQ = H @ W_Q
        HK = H @ W_K
        scores = jnp.einsum('nd,md->nm', HQ, HK)
        scores = scores * A * scale
        attn = jax.nn.softmax(scores, axis=1)
        return attn @ (H @ W_V)

    def _L1_gnn_ref(x, adj, kernels, attn_self, attn_neigh, biases):
        import jax, jax.numpy as jnp
        import numpy as np
        N, DIN, F, H = (4096, 512, 64, 8)
        EPS = float(np.finfo(np.float64).eps)
        mask = (adj > 0).astype(x.dtype)
        outs = []
        for h in range(kernels.shape[0]):
            feats = x @ kernels[h]
            a_s = feats @ attn_self[h]
            a_n = feats @ attn_neigh[h]
            diff = a_s[:, None] - a_n[None, :]
            dense = jnp.exp(-(diff * diff)) * mask
            dense = dense / (dense.sum(axis=1, keepdims=True) + EPS)
            outs.append(dense @ feats + biases[h])
        out = jnp.concatenate(outs, axis=-1)
        return jax.nn.relu(out)

    h = jnp.maximum(_layernorm(x, axis=-1), 0.0)
    x = x + _L0_gnn_ref(h, adj, L0_gnn_W_Q, L0_gnn_W_K, L0_gnn_W_V)
    h = jnp.maximum(_layernorm(x, axis=-1), 0.0)
    x = x + _L1_gnn_ref(h, adj, L1_gnn_kernels, L1_gnn_attn_self, L1_gnn_attn_neigh, L1_gnn_biases)
    return x


_drawn_inputs = setup_inputs


def setup_inputs(seed=0):
    import zlib

    import numpy as np

    out = dict(_drawn_inputs(seed))
    spreads = {'L1_gnn_biases': (0.0, 0.8)}
    factors = {'L0_gnn_W_Q': 8.0,
     'L0_gnn_W_K': 7.871,
     'L1_gnn_kernels': 8.0,
     'L1_gnn_attn_self': 8.0,
     'L1_gnn_attn_neigh': 8.0}
    for name, (base, spread) in spreads.items():
        noise = np.random.default_rng([zlib.crc32(name.encode()), seed]).standard_normal(out[name].shape)
        drawn = base * np.exp(spread * noise) if base else spread * noise
        out[name] = jnp.asarray(drawn.astype(out[name].dtype))
    for name, factor in factors.items():
        out[name] = (out[name] * factor).astype(out[name].dtype)
    return out
```

```python
from contextlib import ExitStack

import numpy as np
import concourse.bass as bass
from concourse import mybir

ALU = mybir.AluOpType
ACT = mybir.ActivationFunctionType
AX = mybir.AxisListType
F32 = mybir.dt.float32
F16 = mybir.dt.float16

P = 128
N, D = 4096, 512
HEADS, F = 8, 64
BLOCKS = N // P
DT = D // P
CHUNK = 512
CHUNKS = N // CHUNK
TPC = CHUNK // P
LN_EPS = 1e-5
SUM_EPS = float(np.finfo(np.float64).eps)
P_SCALE = 2.0 ** 15
G_TOP = 1024.0
G_LEAST = 1e-30
GROUPS = 2
GH = HEADS // GROUPS
MC = 1024
FX = GH * F + 2 * GH
QUERY, GRAPH = "query", "graph"


class RowBlock:

    def __init__(self, pair, offset):
        self.number = 2 * pair + offset
        self.parity = offset % 2
        self.pair = pair + offset // 2


def ge(eng, sem, value):
    if isinstance(value, int) and value <= 0:
        return
    eng.wait_ge(sem, value)


def hold(eng, held):
    eng.sem_inc(held, 1)


def pipeline(eng, step, lag):

    def static(j):
        step(lambda k: RowBlock(j // 2, j % 2 - k) if 0 <= j - k < BLOCKS else None)

    for j in range(4):
        static(j)
    with eng.Fori(2, BLOCKS // 2) as pair:
        for offset in range(2):
            step(lambda k: RowBlock(pair, offset - k))
    for j in range(BLOCKS, BLOCKS + lag):
        static(j)


def open_allocator(nc, stack, prefix):
    def sb(name, shape, dt=F32):
        return stack.enter_context(nc.sbuf_tensor(prefix + name, shape, dt))

    def ps(name, shape=(P, CHUNK)):
        return stack.enter_context(nc.psum_tensor(prefix + name, list(shape), F32))

    def sem(name):
        return stack.enter_context(nc.semaphore(prefix + name))

    return sb, ps, sem


def make_identity(nc, ident):
    with nc.semaphore("ident_zeroed") as zeroed, nc.semaphore("ident_done") as done, nc.Block() as block:

        @block.gpsimd
        def _(pool):
            pool.memset(ident[:, :], 0.0).then_inc(zeroed, 1)
            pool.wait_ge(zeroed, 1)
            pool.affine_select(out=ident[:, :], in_=ident[:, :], compare_op=ALU.not_equal, fill=1.0,
                               base=0, pattern=[[-1, P]], channel_multiplier=1).then_inc(done, 1)
            pool.wait_ge(done, 1)


def fold_query_key(nc, ident, wqT, wkT, m_sb):
    with ExitStack() as stack:
        sb, ps, sem = open_allocator(nc, stack, "m_")
        wq_sb = sb("wq", [P, DT, D])
        wk_sb = sb("wk", [P, DT, D])
        psM = ps("psM")
        loaded, product, copied = sem("loaded"), sem("product"), sem("copied")
        block = stack.enter_context(nc.Block())

        @block.sync
        def _(sp):
            sp.dma_start(wq_sb[:, :, :], wqT.rearrange("(t p) n -> p t n", p=P)).then_inc(loaded, 16)
            sp.dma_start(wk_sb[:, :, :], wkT.rearrange("(t p) n -> p t n", p=P)).then_inc(loaded, 16)

        @block.tensor
        def _(pe):
            pe.wait_ge(loaded, 32)
            for rows in range(DT):
                ge(pe, copied, rows)
                for t in range(DT):
                    mm = pe.matmul(psM[:, :], wq_sb[:, t, rows * P:(rows + 1) * P], wk_sb[:, t, :],
                                   start=(t == 0), stop=(t == DT - 1))
                mm.then_inc(product, 1)

        @block.scalar
        def _(act):
            for rows in range(DT):
                act.wait_ge(product, rows + 1)
                act.activation(m_sb[:, rows, :], psM[:, :], ACT.Copy).then_inc(copied, 1)
            act.wait_ge(copied, DT)


def project_rows(nc, kind, ident, rows, weights, res):
    query = kind == QUERY
    with ExitStack() as stack:
        sb, ps, sem = open_allocator(nc, stack, kind[0] + "_")
        xin = sb("xin", [P, 2, D])
        stats = sb("stats", [P, 6])
        mv = sb("mv", [P, 2])
        var = sb("var", [P, 1])
        std = sb("std", [P, 1])
        r0 = sb("r0", [P, 1])
        vrr = sb("vrr", [P, 1])
        corr = sb("corr", [P, 1])
        rstd = sb("rstd", [P, 2])
        shift = sb("shift", [P, 2])
        h = sb("h", [P, 2, D])
        hT = sb("hT", [P, 2, D])
        psT, psY = ps("psT"), ps("psY")
        x_loaded = [sem("x_loaded0"), sem("x_loaded1")]
        w_loaded = sem("w_loaded")
        dve_stat = sem("dve_stat")
        var_ready, std_ready = sem("var_ready"), sem("std_ready")
        norm_ready, h_ready = sem("norm_ready"), sem("h_ready")
        hT_ready, hT_copied, y_ready = sem("hT_ready"), sem("hT_copied"), sem("y_ready")
        stored = [sem("stored0"), sem("stored1")]
        if query:
            gtop = sb("gtop", [P, 1])
            gunit = sb("gunit", [P, 1])
            ginv = sb("ginv", [P, 1])
            gs = sb("gs", [P, D])
            gT = sb("gT", [P, 2, 2, D], F16)
            psG = ps("psG")
            g_step = sem("g_step")
            gs_ready, gT_ready = sem("gs_ready"), sem("gT_ready")
            gT_high, gT_low = sem("gT_high"), sem("gT_low")
            hT_high, hT_low = sem("hT_high"), sem("hT_low")
            h_high, h_low = sem("h_high"), sem("h_low")
        else:
            asn = sb("asn", [P, 2, D])
            fx = sb("fx", [P, 2, GROUPS, FX])
            s_all = sb("s_all", [P, HEADS, BLOCKS])
            sT = sb("sT", [P, 2, P])
            prod = sb("prod", [P, 2, D])
            feats_copied, prod_ready, sn_ready = sem("feats_copied"), sem("prod_ready"), sem("sn_ready")
            record_ready = sem("record_ready")
            sT_ready, sT_copied, s_stored = sem("sT_ready"), sem("sT_copied"), sem("s_stored")
        held, held_store = sem("held"), sem("held_store")
        block = stack.enter_context(nc.Block())
        x_rows = rows.rearrange("(b p) d -> b p d", p=P)

        @block.sync
        def _(sp):
            if not query:
                sp.dma_start(weights, res["w_dram"].rearrange("(t p) n -> p t n", p=P)).then_inc(w_loaded, 16)
                for i, name in enumerate(("attn_self", "attn_neigh")):
                    sp.dma_start(asn[:, i, :], res[name].partition_broadcast(P)).then_inc(w_loaded, 16)

            def step(at):
                b = at(0)
                ge(sp, h_ready, b.number - 1)
                sp.dma_start(xin[:, b.parity, :], x_rows[b.number]).then_inc(x_loaded[b.parity], 16)

            pipeline(sp, step, 0)

        @block.scalar
        def _(act):
            def step(at):
                b, a = at(0), at(1)
                if b:
                    act.wait_ge(var_ready, b.number + 1)
                    act.activation(std[:, :], var[:, :], ACT.Sqrt).then_inc(std_ready, 1)
                    act.wait_ge(norm_ready, b.number + 1)
                    ge(act, hT_ready, b.number - 1)
                    if query:
                        ge(act, h_low, b.number - 1)
                    act.activation(h[:, b.parity, :], xin[:, b.parity, :], ACT.Relu,
                                   bias=shift[:, b.parity:b.parity + 1],
                                   scale=rstd[:, b.parity:b.parity + 1]).then_inc(h_ready, 1)
                    act.wait_ge(hT_ready, b.number + 1)
                    ge(act, y_ready, b.number - 1)
                    if query:
                        ge(act, hT_low, b.number - 1)
                    act.activation(hT[:, b.parity, :], psT[:, :], ACT.Copy).then_inc(hT_copied, 1)
                if a and query:
                    act.wait_ge(gT_ready, a.number + 1)
                    ge(act, stored[a.parity], 16 * a.pair)
                    act.activation(gT[:, a.parity, 0, :], psG[:, :], ACT.Copy).then_inc(gT_high, 1)
                if a and not query:
                    act.wait_ge(y_ready, a.number + 1)
                    ge(act, stored[a.parity], 16 * a.pair)
                    act.activation(fx[:, a.parity, :, 0:GH * F], psY[:, :].rearrange("p (g f) -> p g f", g=GROUPS),
                                   ACT.Copy).then_inc(feats_copied, 1)

            pipeline(act, step, 1)
            if not query:
                for half in range(2):
                    act.wait_ge(sT_ready, 2)
                    act.activation(sT[:, half, :], psT[:, half * P:(half + 1) * P], ACT.Copy).then_inc(sT_copied, 1)

        @block.tensor
        def _(pe):
            ge(pe, w_loaded, 0 if query else 48)

            def step(at):
                b, a = at(0), at(1)
                if b:
                    pe.wait_ge(h_ready, b.number + 1)
                    ge(pe, hT_copied, b.number)
                    for t in range(DT):
                        mm = pe.transpose(psT[:, t * P:(t + 1) * P], h[:, b.parity, t * P:(t + 1) * P], ident[:, :])
                    mm.then_inc(hT_ready, 1)
                if a and query:
                    pe.wait_ge(gs_ready, a.number + 1)
                    ge(pe, gT_low, a.number)
                    for t in range(DT):
                        mm = pe.transpose(psG[:, t * P:(t + 1) * P], gs[:, t * P:(t + 1) * P], ident[:, :])
                    mm.then_inc(gT_ready, 1)
                if b:
                    pe.wait_ge(hT_copied, b.number + 1)
                    ge(pe, gs_ready if query else feats_copied, b.number)
                    for t in range(DT):
                        mm = pe.matmul(psY[:, :], hT[:, b.parity, t * P:(t + 1) * P], weights[:, t, :],
                                       start=(t == 0), stop=(t == DT - 1))
                    mm.then_inc(y_ready, 1)

            pipeline(pe, step, 1)
            if not query:
                pe.wait_ge(sn_ready, 2 * BLOCKS)
                pe.wait_ge(hT_copied, BLOCKS)
                s_cols = s_all[:, :, :].rearrange("p h b -> p (h b)")
                for half in range(2):
                    pe.transpose(psT[:, half * P:(half + 1) * P], s_cols[:, half * P:(half + 1) * P],
                                 ident[:, :]).then_inc(sT_ready, 1)

        @block.gpsimd
        def _(pool):
            def step(at):
                b, a = at(0), at(1)
                if b and query:
                    pool.wait_ge(h_ready, b.number + 1)
                    pool.tensor_copy(res["h_hi"][:, b.number, :], h[:, b.parity, :]).then_inc(h_high, 1)
                    pool.wait_ge(h_high, b.number + 1)
                    pool.tensor_tensor(res["h_lo"][:, b.number, :], h[:, b.parity, :],
                                       res["h_hi"][:, b.number, :], ALU.subtract).then_inc(h_low, 1)
                if a and query:
                    pool.wait_ge(gT_low, a.number + 1)
                    pool.wait_ge(gT_high, a.number + 1)
                    hold(pool, held_store)
                    pool.dma_start(res["g_dram"][a.number], gT[:, a.parity, :, :]).then_inc(stored[a.parity], 16)
                if a and not query:
                    pool.wait_ge(feats_copied, a.number + 1)
                    pool.wait_ge(record_ready, a.number + 1)
                    hold(pool, held_store)
                    pool.dma_start(res["fx_dram"][a.number], fx[:, a.parity, :, :]).then_inc(stored[a.parity], 16)

            pipeline(pool, step, 1)
            if query:
                pool.wait_ge(h_low, BLOCKS)
            for s in stored:
                pool.wait_ge(s, 16 * BLOCKS // 2)
            if not query:
                pool.wait_ge(sT_copied, 2)
                pool.dma_start(res["s_dram"].rearrange("(i q) m -> q i m", i=2), sT[:, :, :]).then_inc(s_stored, 16)
                pool.wait_ge(s_stored, 16)

        @block.vector
        def _(dve):
            SMALL = 6

            def step(at):
                b, a = at(0), at(1)
                if b:
                    n = b.number
                    dve.wait_ge(x_loaded[b.parity], 16 * (b.pair + 1))
                    dve.bn_stats(stats[:, :], xin[:, b.parity, :]).then_inc(dve_stat, 1)
                    dve.wait_ge(dve_stat, SMALL * n + 1)
                    hold(dve, held)
                    dve.bn_aggr(mv[:, :], stats[:, :]).then_inc(dve_stat, 1)
                    dve.wait_ge(dve_stat, SMALL * n + 2)
                    dve.tensor_scalar(var[:, :], mv[:, 1:2], LN_EPS, None, ALU.add).then_inc(var_ready, 1)
                    dve.wait_ge(std_ready, n + 1)
                    dve.reciprocal(r0[:, :], std[:, :]).then_inc(dve_stat, 1)
                    dve.wait_ge(dve_stat, SMALL * n + 3)
                    dve.scalar_tensor_tensor(out=vrr[:, :], in0=r0[:, :], scalar=var[:, :], in1=r0[:, :],
                                             op0=ALU.mult, op1=ALU.mult).then_inc(dve_stat, 1)
                    dve.wait_ge(dve_stat, SMALL * n + 4)
                    dve.tensor_scalar(corr[:, :], vrr[:, :], -0.5, 1.5, ALU.mult, ALU.add).then_inc(dve_stat, 1)
                    dve.wait_ge(dve_stat, SMALL * n + 5)
                    dve.tensor_tensor(rstd[:, b.parity:b.parity + 1], r0[:, :], corr[:, :], ALU.mult).then_inc(dve_stat, 1)
                    dve.wait_ge(dve_stat, SMALL * n + 6)
                    dve.scalar_tensor_tensor(out=shift[:, b.parity:b.parity + 1], in0=mv[:, 0:1], scalar=-1.0,
                                             in1=rstd[:, b.parity:b.parity + 1],
                                             op0=ALU.mult, op1=ALU.mult).then_inc(norm_ready, 1)
                if a and query:
                    n = a.number
                    dve.wait_ge(y_ready, n + 1)
                    ge(dve, gs_ready, n)
                    dve.tensor_reduce(gtop[:, :], psY[:, :], AX.X, ALU.max,
                                      apply_absolute_value=True).then_inc(g_step, 1)
                    dve.wait_ge(g_step, 3 * n + 1)
                    dve.tensor_scalar(gunit[:, :], gtop[:, :], G_LEAST, 1.0 / G_TOP, ALU.max, ALU.mult).then_inc(g_step, 1)
                    dve.wait_ge(g_step, 3 * n + 2)
                    dve.tensor_scalar(res["row_scale"][:, bass.ds(n, 1)], gunit[:, :], float(D) ** -0.5, None, ALU.mult)\
                       .then_inc(res["row_scale_ready"], 1)
                    dve.reciprocal(ginv[:, :], gunit[:, :]).then_inc(g_step, 1)
                    dve.wait_ge(g_step, 3 * n + 3)
                    ge(dve, gT_ready, n)
                    dve.tensor_scalar(gs[:, :], psY[:, :], ginv[:, :], None, ALU.mult).then_inc(gs_ready, 1)
                if b and query:
                    n = b.number
                    dve.wait_ge(hT_copied, n + 1)
                    src = hT[:, b.parity, :].rearrange("p (t q) -> p t q", t=DT)
                    dve.tensor_copy(res["hT_hi"][:, :, n, :], src).then_inc(hT_high, 1)
                    dve.wait_ge(hT_high, n + 1)
                    dve.tensor_tensor(res["hT_lo"][:, :, n, :], src, res["hT_hi"][:, :, n, :],
                                      ALU.subtract).then_inc(hT_low, 1)
                if a and query:
                    n = a.number
                    dve.wait_ge(gT_high, n + 1)
                    dve.tensor_tensor(gT[:, a.parity, 1, :], psG[:, :], gT[:, a.parity, 0, :],
                                      ALU.subtract).then_inc(gT_low, 1)
                if a and not query:
                    n = a.number
                    if isinstance(n, int) and n == 0:
                        dve.wait_ge(w_loaded, 48)
                    dve.wait_ge(feats_copied, n + 1)
                    feats = fx[:, a.parity, :, 0:GH * F]
                    for i in range(2):
                        dve.tensor_tensor(prod[:, i, :].rearrange("p (g f) -> p g f", g=GROUPS), feats,
                                          asn[:, i, :].rearrange("p (g f) -> p g f", g=GROUPS),
                                          ALU.mult).then_inc(prod_ready, 1)
                    dve.wait_ge(prod_ready, 2 * n + 1)
                    dve.tensor_reduce(s_all[:, :, n], prod[:, 0, :].rearrange("p (h f) -> p h f", h=HEADS),
                                      AX.X, ALU.add).then_inc(sn_ready, 1)
                    dve.wait_ge(prod_ready, 2 * n + 2)
                    dve.tensor_reduce(fx[:, a.parity, :, GH * F + GH:FX],
                                      prod[:, 1, :].rearrange("p (g h f) -> p g h f", g=GROUPS, h=GH),
                                      AX.X, ALU.add).then_inc(sn_ready, 1)
                    dve.wait_ge(sn_ready, 2 * n + 2)
                    dve.tensor_scalar(fx[:, a.parity, :, GH * F:GH * F + GH],
                                      fx[:, a.parity, :, GH * F + GH:FX], -1.0, None, ALU.mult).then_inc(record_ready, 1)

            pipeline(dve, step, 1)


def attend(nc, ident, res):
    with ExitStack() as stack:
        sb, ps, sem = open_allocator(nc, stack, "a_")
        wv = sb("wv", [P, DT, D])
        adj = sb("adj", [P, N])
        scores = sb("scores", [P, N])
        pT_hi = sb("pT_hi", [P, N], F16)
        pT_lo = sb("pT_lo", [P, N], F16)
        gT = sb("gT", [P, 2, 2, D], F16)
        row_scale = sb("row_scale", [P, 2])
        maxes = sb("maxes", [P, CHUNKS])
        neg_max = sb("neg_max", [P, 2])
        sums = sb("sums", [P, 2])
        recip = sb("recip", [P, 1])
        mean_h = sb("mean_h", [P, D])
        mean_hT = sb("mean_hT", [P, D])
        x_in = sb("x_in", [P, D])
        x1_out = sb("x1_out", [P, D])
        psS = [ps("psS0"), ps("psS1")]
        psT = [ps("psT0"), ps("psT1")]
        psU, psV, psY = ps("psU"), ps("psV"), ps("psY")
        wv_loaded, x_loaded, x1_stored = sem("wv_loaded"), sem("x_loaded"), sem("x1_stored")
        adj_loaded = [sem(f"adj_loaded{q}") for q in range(CHUNKS // 2)]
        g_loaded = [sem("g_loaded0"), sem("g_loaded1")]
        scale_ready = sem("scale_ready")
        scores_ready, scores_taken = sem("scores_ready"), sem("scores_taken")
        neg_ready, exp_ready = sem("neg_ready"), sem("exp_ready")
        pT_ready, pT_high, pT_low = sem("pT_ready"), sem("pT_high"), sem("pT_low")
        u_ready, recip_ready, mean_ready = sem("u_ready"), sem("recip_ready"), sem("mean_ready")
        meanT_ready, meanT_copied = sem("meanT_ready"), sem("meanT_copied")
        y_ready, x1_ready = sem("y_ready"), sem("x1_ready")
        held, held_store = sem("held"), sem("held_store")
        block = stack.enter_context(nc.Block())
        adj_rows = res["adj"].rearrange("(b p) m -> b p m", p=P)
        x_rows = res["x"].rearrange("(b p) d -> b p d", p=P)
        x1_rows = res["x1_dram"].rearrange("(b p) d -> b p d", p=P)

        @block.sync
        def _(sp):
            sp.dma_start(wv[:, :, :], res["w_v"].rearrange("(t p) n -> p t n", p=P)).then_inc(wv_loaded, 16)

            def step(at):
                b = at(0)
                ge(sp, scores_ready, CHUNKS * (b.number - 1))
                sp.dma_start(gT[:, b.parity, :, :], res["g_dram"][b.number]).then_inc(g_loaded[b.parity], 16)
                for q in range(CHUNKS // 2):
                    ge(sp, scores_taken, CHUNKS * (b.number - 1) + 2 * q + 2)
                    cols = slice(2 * q * CHUNK, (2 * q + 2) * CHUNK)
                    sp.dma_start(adj[:, cols], adj_rows[b.number, :, cols]).then_inc(adj_loaded[q], 16)

            pipeline(sp, step, 0)

        @block.gpsimd
        def _(pool):
            def step(at):
                a = at(2)
                if a:
                    ge(pool, x1_ready, a.number)
                    pool.wait_ge(mean_ready, a.number + 1)
                    hold(pool, held_store)
                    pool.dma_start(x_in[:, :], x_rows[a.number]).then_inc(x_loaded, 16)
                    pool.wait_ge(x1_ready, a.number + 1)
                    hold(pool, held_store)
                    pool.dma_start(x1_rows[a.number], x1_out[:, :]).then_inc(x1_stored, 16)

            pipeline(pool, step, 2)
            pool.wait_ge(x1_stored, 16 * BLOCKS)

        @block.tensor
        def _(pe):
            def transpose_p(a, c):
                if c == 0:
                    pe.wait_ge(exp_ready, a.number + 1)
                ge(pe, pT_low, CHUNKS * a.number + c - 1)
                for t in range(TPC):
                    col = c * CHUNK + t * P
                    mm = pe.transpose(psT[c % 2][:, t * P:(t + 1) * P], scores[:, col:col + P], ident[:, :])
                mm.then_inc(pT_ready, 1)

            def score(b, c):
                if c == 0:
                    pe.wait_ge(g_loaded[b.parity], 16 * (b.pair + 1))
                ge(pe, scores_taken, CHUNKS * b.number + c - 1)
                parts = [(g, t, hT) for t in range(DT) for g, hT in ((1, "hT_hi"), (0, "hT_lo"), (0, "hT_hi"))]
                for i, (g, t, hT) in enumerate(parts):
                    mm = pe.matmul(psS[c % 2][:, :], gT[:, b.parity, g, t * P:(t + 1) * P],
                                   res[hT][:, t, c * TPC:(c + 1) * TPC, :],
                                   start=(i == 0), stop=(i == len(parts) - 1))
                mm.then_inc(scores_ready, 1)

            def weighted_mean(a):
                ge(pe, mean_ready, a.number)
                for k in range(BLOCKS):
                    if k % TPC == 0:
                        pe.wait_ge(pT_low, CHUNKS * a.number + k // TPC + 1)
                    for i, (pT, h) in enumerate(((pT_lo, "h_hi"), (pT_hi, "h_lo"), (pT_hi, "h_hi"))):
                        mm = pe.matmul(psU[:, :], pT[:, k * P:(k + 1) * P], res[h][:, k, :],
                                       start=(k == 0 and i == 0), stop=(k == BLOCKS - 1 and i == 2))
                mm.then_inc(u_ready, 1)

            def step(at):
                b, a, z = at(0), at(1), at(2)
                for c in range(CHUNKS):
                    if a:
                        transpose_p(a, c)
                    if b:
                        score(b, c)
                    if z and c == 1:
                        pe.wait_ge(mean_ready, z.number + 1)
                        ge(pe, meanT_copied, z.number)
                        for t in range(DT):
                            mm = pe.transpose(psV[:, t * P:(t + 1) * P], mean_h[:, t * P:(t + 1) * P], ident[:, :])
                        mm.then_inc(meanT_ready, 1)
                    if z and c == 3:
                        if isinstance(z.number, int) and z.number == 0:
                            pe.wait_ge(wv_loaded, 16)
                        pe.wait_ge(meanT_copied, z.number + 1)
                        ge(pe, x1_ready, z.number)
                        for t in range(DT):
                            mm = pe.matmul(psY[:, :], mean_hT[:, t * P:(t + 1) * P], wv[:, t, :],
                                           start=(t == 0), stop=(t == DT - 1))
                        mm.then_inc(y_ready, 1)
                if a:
                    weighted_mean(a)

            pipeline(pe, step, 2)

        @block.scalar
        def _(act):
            def step(at):
                b, a, z = at(0), at(1), at(2)
                for c in range(CHUNKS):
                    if a:
                        act.wait_ge(pT_ready, CHUNKS * a.number + c + 1)
                        act.activation(pT_hi[:, c * CHUNK:(c + 1) * CHUNK], psT[c % 2][:, :], ACT.Copy,
                                       scale=P_SCALE).then_inc(pT_high, 1)
                    if z and c == 1:
                        act.wait_ge(meanT_ready, z.number + 1)
                        act.activation(mean_hT[:, :], psV[:, :], ACT.Copy).then_inc(meanT_copied, 1)
                if b:
                    act.wait_ge(neg_ready, b.number + 1)
                    act.activation(scores[:, :], scores[:, :], ACT.Exp, bias=neg_max[:, b.parity:b.parity + 1],
                                   accum_out=sums[:, b.parity:b.parity + 1]).then_inc(exp_ready, 1)

            pipeline(act, step, 2)

        @block.vector
        def _(dve):
            def step(at):
                b, a, z = at(0), at(1), at(2)
                if b:
                    ge(dve, scores_taken, CHUNKS * (b.number - 1))
                    dve.tensor_copy(row_scale[:, b.parity:b.parity + 1], res["row_scale"][:, bass.ds(b.number, 1)]
                                    ).then_inc(scale_ready, 1)
                    dve.wait_ge(scale_ready, b.number + 1)
                for c in range(CHUNKS):
                    cols = slice(c * CHUNK, (c + 1) * CHUNK)
                    if a:
                        dve.wait_ge(pT_high, CHUNKS * a.number + c + 1)
                        dve.scalar_tensor_tensor(out=pT_lo[:, cols], in0=psT[c % 2][:, :], scalar=P_SCALE,
                                                 in1=pT_hi[:, cols], op0=ALU.mult, op1=ALU.subtract
                                                 ).then_inc(pT_low, 1)
                    if b:
                        dve.wait_ge(adj_loaded[c // 2], 16 * (b.number + 1))
                        if c == 0:
                            ge(dve, neg_ready, b.number)
                        dve.wait_ge(scores_ready, CHUNKS * b.number + c + 1)
                        hold(dve, held)
                        dve.tensor_tensor_reduce(out=scores[:, cols], in0=psS[c % 2][:, :], in1=adj[:, cols],
                                                 scale=row_scale[:, b.parity:b.parity + 1], scalar=-3.0e38,
                                                 op0=ALU.mult, op1=ALU.max, accum_out=maxes[:, c:c + 1]
                                                 ).then_inc(scores_taken, 1)
                    if z and c == 3:
                        dve.wait_ge(y_ready, z.number + 1)
                        dve.wait_ge(x_loaded, 16 * (z.number + 1))
                        ge(dve, x1_stored, 16 * z.number)
                        dve.tensor_tensor(x1_out[:, :], psY[:, :], x_in[:, :], ALU.add).then_inc(x1_ready, 1)
                if b:
                    dve.wait_ge(scores_taken, CHUNKS * (b.number + 1))
                    dve.tensor_reduce(neg_max[:, b.parity:b.parity + 1], maxes[:, :], AX.X, ALU.max,
                                      negate=True).then_inc(neg_ready, 1)
                if a:
                    dve.wait_ge(exp_ready, a.number + 1)
                    dve.reciprocal(recip[:, :], sums[:, a.parity:a.parity + 1]).then_inc(recip_ready, 1)
                    dve.wait_ge(recip_ready, a.number + 1)
                    dve.wait_ge(u_ready, a.number + 1)
                    ge(dve, meanT_ready, a.number)
                    dve.tensor_scalar(mean_h[:, :], psU[:, :], recip[:, :], 1.0 / P_SCALE, ALU.mult, ALU.mult
                                      ).then_inc(mean_ready, 1)

            pipeline(dve, step, 2)


def aggregate(nc, ident, res):
    KS = 2
    MT = MC // P
    HALVES = MC // CHUNK
    PAIRS = GH // 2
    with ExitStack() as stack:
        sb, ps, sem = open_allocator(nc, stack, "w_")
        adjT = sb("adjT", [P, KS, MC])
        mask = sb("mask", [P, MC])
        fx = sb("fx", [P, KS, FX])
        s_rows = sb("s_rows", [P, 2, GH, MC])
        w = sb("w", [P, KS, GH, MC])
        zeros = sb("zeros", [P, CHUNK], F16)
        ones = sb("ones", [P, 32])
        bias = sb("bias", [P, HEADS * F])
        outT = sb("outT", [P, PAIRS + 1, MC])
        x1 = sb("x1", [P, MT, GH * F])
        y = sb("y", [P, MT, GH * F])
        recip = sb("recip", [P, MT, GH])
        psO = [[ps(f"psO{p}{half}") for half in range(HALVES)] for p in range(PAIRS)]
        psR = [ps(f"psR{half}") for half in range(HALVES)]
        psN = [ps("psN0"), ps("psN1")]
        k_loaded = [sem("k_loaded0"), sem("k_loaded1")]
        s_loaded, bias_loaded, x1_loaded = sem("s_loaded"), sem("bias_loaded"), sem("x1_loaded")
        const_ready = sem("const_ready")
        squared, exped, diff_ready, mask_ready = sem("squared"), sem("exped"), sem("diff_ready"), sem("mask_ready")
        pool_squared, dve_masked, pool_masked = sem("pool_squared"), sem("dve_masked"), sem("pool_masked")
        w_used = sem("w_used")
        outT_copied, nat_ready, nat_taken = sem("outT_copied"), sem("nat_ready"), sem("nat_taken")
        eps_added, recip_ready, biased, y_ready = sem("eps_added"), sem("recip_ready"), sem("biased"), sem("y_ready")
        y_stored = sem("y_stored")
        block = stack.enter_context(nc.Block())
        adjT_view = res["adjT"].rearrange("(b p) (c m) -> b c p m", p=P, m=MC)
        s_view = res["s_dram"].rearrange("(g h b) m -> g h (b m)", g=GROUPS, h=GH)
        x1_view = res["x1_dram"].rearrange("(c t p) (g d) -> c g p t d", t=MT, p=P, g=GROUPS)
        y_view = res["out"].rearrange("(c t p) (g d) -> c g p t d", t=MT, p=P, g=GROUPS)

        BANKS = (PAIRS + 1) * HALVES

        def sweep(eng, step, first=None, middle=None, last=None):
            def part(c, group):
                o = GROUPS * c + group
                turns = BLOCKS // KS
                if first:
                    first(o, c, group)
                for begin in (0, turns // 2):
                    if begin and middle and not (isinstance(o, int) and o == 0):
                        middle(o, group)
                    with eng.Fori(begin, begin + turns // 2) as turn:
                        for slot in range(KS):
                            u = turns * o + turn
                            step(o, c, group, KS * turn + slot, slot, u, KS * u + slot)
                if last:
                    last(o)

            for group in range(GROUPS):
                part(0, group)
            with eng.Fori(1, N // MC) as c:
                for group in range(GROUPS):
                    part(c, group)

        PARTS = GROUPS * (N // MC)

        @block.sync
        def _(sp):
            sp.dma_start(bias[:, :], res["biases"].partition_broadcast(P)).then_inc(bias_loaded, 16)

            def store_y(q, c, group):
                sp.wait_ge(y_ready, q + 1)
                sp.dma_start(y_view[c, group], y[:, :, :]).then_inc(y_stored, 16)

            def load_x1(q, c, group):
                ge(sp, y_ready, q)
                sp.dma_start(x1[:, :, :], x1_view[c, group]).then_inc(x1_loaded, 16)

            def first(o, c, group):
                if not (isinstance(o, int) and o < 2):
                    store_y(o - 2, c - 1, group)
                if not (isinstance(o, int) and o < 1):
                    load_x1(o - 1, c - 1 + group, 1 - group)
                ge(sp, w_used, KS + BLOCKS * (o - 1) if not (isinstance(o, int) and o < 2) else 0)
                sp.dma_start(s_rows[:, group, :, :],
                             s_view[group, :, bass.ds(c * MC, MC)].partition_broadcast(P)).then_inc(s_loaded, 16)

            def step(o, c, group, k, slot, u, g):
                sp.wait_ge(w_used, g + 1)
                sp.dma_start(adjT[:, slot, :], adjT_view[k, c]).then_inc(k_loaded[slot], 16)
                sp.dma_start(fx[:, slot, :], res["fx_dram"][k, :, group, :]).then_inc(k_loaded[slot], 16)

            sweep(sp, step, first)
            store_y(PARTS - 2, N // MC - 1, 0)
            load_x1(PARTS - 1, N // MC - 1, 1)
            store_y(PARTS - 1, N // MC - 1, 1)
            sp.wait_ge(y_stored, 16 * PARTS)

        @block.scalar
        def _(act):
            def square(group, slot, a):
                act.activation(w[:, slot, a, :], s_rows[:, group, a, :], ACT.Square,
                               bias=fx[:, slot, GH * F + a:GH * F + a + 1]).then_inc(squared, 1)

            def step(o, c, group, k, slot, u, g):
                act.wait_ge(s_loaded, 16 * (o + 1))
                act.wait_ge(k_loaded[slot], 32 * (u + 1))
                act.wait_ge(w_used, g + 1)
                square(group, slot, 0)
                square(group, slot, 1)
                act.wait_ge(squared, 3 * g + 2)
                act.activation(w[:, slot, 0:2, :], w[:, slot, 0:2, :], ACT.Exp, scale=-1.0).then_inc(exped, 1)
                square(group, slot, 2)
                act.wait_ge(squared, 3 * g + 3)
                act.wait_ge(pool_squared, g + 1)
                act.activation(w[:, slot, 2:4, :], w[:, slot, 2:4, :], ACT.Exp, scale=-1.0).then_inc(exped, 1)

            sweep(act, step)

        @block.gpsimd
        def _(pool):
            pool.memset(zeros[:, :], 0.0).then_inc(const_ready, 1)
            pool.memset(ones[:, :], 1.0).then_inc(const_ready, 1)
            pool.sem_inc(pool_masked, 1)

            def step(o, c, group, k, slot, u, g):
                pool.wait_ge(diff_ready, g + 1)
                pool.tensor_tensor(w[:, slot, 3, :], w[:, slot, 3, :], w[:, slot, 3, :], ALU.mult).then_inc(pool_squared, 1)
                pool.wait_ge(exped, 2 * g + 2)
                pool.wait_ge(mask_ready, g + 1)
                pool.tensor_tensor(w[:, slot, 3, :], w[:, slot, 3, :], mask[:, :], ALU.mult).then_inc(pool_masked, 1)

            sweep(pool, step)

        @block.vector
        def _(dve):
            def step(o, c, group, k, slot, u, g):
                dve.wait_ge(s_loaded, 16 * (o + 1))
                dve.wait_ge(k_loaded[slot], 32 * (u + 1))
                dve.wait_ge(w_used, g + 1)
                n_at = GH * F + GH + 3
                dve.tensor_scalar(w[:, slot, 3, :], s_rows[:, group, 3, :], fx[:, slot, n_at:n_at + 1], None,
                                  ALU.subtract).then_inc(diff_ready, 1)
                dve.wait_ge(exped, 2 * g + 1)
                dve.scalar_tensor_tensor(out=w[:, slot, 0:2, :],
                                         in0=adjT[:, slot, :].unsqueeze(1).broadcast_to([P, 2, MC]), scalar=0.0,
                                         in1=w[:, slot, 0:2, :], op0=ALU.is_gt, op1=ALU.mult).then_inc(dve_masked, 1)
                dve.wait_ge(pool_masked, g + 1)
                dve.tensor_scalar(mask[:, :], adjT[:, slot, :], 0.0, None, ALU.is_gt).then_inc(mask_ready, 1)
                dve.wait_ge(exped, 2 * g + 2)
                dve.scalar_tensor_tensor(out=w[:, slot, 2, :], in0=adjT[:, slot, :], scalar=0.0,
                                         in1=w[:, slot, 2, :], op0=ALU.is_gt, op1=ALU.mult).then_inc(dve_masked, 1)

            def last(o):
                dve.wait_ge(w_used, KS + BLOCKS * (o + 1))
                ge(dve, nat_ready, MT * o)
                for i, banks in enumerate(psO + [psR]):
                    for half in range(HALVES):
                        dve.tensor_copy(outT[:, i, half * CHUNK:(half + 1) * CHUNK], banks[half][:, :]
                                        ).then_inc(outT_copied, 1)

            def finish(q):
                ge(dve, y_stored, 16 * q)
                for t in range(MT):
                    nat = psN[t % 2]
                    n = MT * q + t
                    dve.wait_ge(nat_ready, n + 1)
                    sums = nat[:, PAIRS * P:(PAIRS + 1) * P].rearrange("p (a r) -> p a r", a=GH)[:, :, 0]
                    dve.tensor_scalar(recip[:, t, :], sums, SUM_EPS, None, ALU.add).then_inc(eps_added, 1)
                    dve.wait_ge(eps_added, n + 1)
                    dve.reciprocal(recip[:, t, :], recip[:, t, :]).then_inc(recip_ready, 1)
                    dve.wait_ge(recip_ready, n + 1)
                    dve.tensor_tensor(y[:, t, :].rearrange("p (a f) -> p a f", a=GH),
                                      nat[:, 0:PAIRS * P].rearrange("p (a f) -> p a f", a=GH),
                                      recip[:, t, :].unsqueeze(2).broadcast_to([P, GH, F]), ALU.mult
                                      ).then_inc(nat_taken, 1)
                dve.wait_ge(nat_taken, MT * (q + 1))

            def add_bias_and_x1(q, group):
                columns = bias[:, group * GH * F:(group + 1) * GH * F]
                dve.tensor_tensor(y[:, :, :], y[:, :, :], columns.unsqueeze(1).broadcast_to([P, MT, GH * F]),
                                  ALU.add).then_inc(biased, 1)
                dve.wait_ge(biased, q + 1)
                dve.wait_ge(x1_loaded, 16 * (q + 1))
                dve.scalar_tensor_tensor(out=y[:, :, :], in0=y[:, :, :], scalar=0.0, in1=x1[:, :, :],
                                         op0=ALU.max, op1=ALU.add).then_inc(y_ready, 1)

            def middle(o, group):
                finish(o - 1)
                add_bias_and_x1(o - 1, 1 - group)

            dve.wait_ge(bias_loaded, 16)
            sweep(dve, step, middle=middle, last=last)
            finish(PARTS - 1)
            add_bias_and_x1(PARTS - 1, 1)

        @block.tensor
        def _(pe):
            pe.sem_inc(w_used, KS)
            pe.wait_ge(const_ready, 2)

            def first(o, c, group):
                ge(pe, outT_copied, BANKS * o)
                for bank in psO[0] + psO[1] + psR:
                    pe.matmul(bank[:, :], zeros[:, 0:P], zeros[:, :], start=True, stop=False, skip_group_check=True)

            def step(o, c, group, k, slot, u, g):
                for pair in range(PAIRS):
                    if pair == 0:
                        pe.wait_ge(dve_masked, 2 * g + 1)
                    else:
                        pe.wait_ge(dve_masked, 2 * g + 2)
                        pe.wait_ge(pool_masked, g + 2)
                    for half in range(HALVES):
                        for i in range(2):
                            a = 2 * pair + i
                            pe.matmul(psO[pair][half][F * i:F * i + F, :], fx[:, slot, F * a:F * a + F],
                                      w[:, slot, a, half * CHUNK:(half + 1) * CHUNK],
                                      start=False, stop=False, skip_group_check=True)
                for half in range(HALVES):
                    for a in range(GH):
                        mm = pe.matmul(psR[half][32 * a:32 * a + 32, :], ones[:, :],
                                       w[:, slot, a, half * CHUNK:(half + 1) * CHUNK],
                                       start=False, stop=False, skip_group_check=True)
                mm.then_inc(w_used, 1)

            def turn_back(q):
                pe.wait_ge(outT_copied, BANKS * (q + 1))
                for t in range(MT):
                    ge(pe, nat_taken, MT * q + t - 1)
                    for i in range(PAIRS + 1):
                        mm = pe.transpose(psN[t % 2][:, i * P:(i + 1) * P], outT[:, i, t * P:(t + 1) * P], ident[:, :])
                    mm.then_inc(nat_ready, 1)

            def middle(o, group):
                turn_back(o - 1)

            sweep(pe, step, first=first, middle=middle)
            turn_back(PARTS - 1)


def program(nc, x, adj, adjT, wqT, wkT, wv, wk1, attn_self, attn_neigh, biases, out):
    g_dram = nc.dram_tensor("g_dram", [BLOCKS, P, 2, D], F16).ap()
    x1_dram = nc.dram_tensor("x1_dram", [N, D], F32).ap()
    fx_dram = nc.dram_tensor("fx_dram", [BLOCKS, P, GROUPS, FX], F32).ap()
    s_dram = nc.dram_tensor("s_dram", [HEADS * BLOCKS, P], F32).ap()
    with nc.sbuf_tensor("ident", [P, P], F32) as ident:
        make_identity(nc, ident)
        with ExitStack() as stack:
            def resident(name, shape, dt):
                return stack.enter_context(nc.sbuf_tensor(name, shape, dt))

            res = {"x": x, "adj": adj, "w_v": wv, "g_dram": g_dram, "x1_dram": x1_dram,
                   "h_hi": resident("h_hi", [P, BLOCKS, D], F16), "h_lo": resident("h_lo", [P, BLOCKS, D], F16),
                   "hT_hi": resident("hT_hi", [P, DT, BLOCKS, P], F16),
                   "hT_lo": resident("hT_lo", [P, DT, BLOCKS, P], F16),
                   "row_scale": resident("row_scales", [P, BLOCKS], F32)}
            with nc.sbuf_tensor("m_sb", [P, DT, D], F32) as m_sb, nc.semaphore("row_scale_ready") as ready:
                fold_query_key(nc, ident, wqT, wkT, m_sb)
                res["row_scale_ready"] = ready
                project_rows(nc, QUERY, ident, x, m_sb, res)
            attend(nc, ident, res)
        with nc.sbuf_tensor("wk1_sb", [P, DT, D], F32) as wk1_sb:
            project_rows(nc, GRAPH, ident, x1_dram, wk1_sb[:, :, :],
                         {"w_dram": wk1, "attn_self": attn_self, "attn_neigh": attn_neigh,
                          "fx_dram": fx_dram, "s_dram": s_dram})
        aggregate(nc, ident, {"adjT": adjT, "fx_dram": fx_dram, "s_dram": s_dram, "x1_dram": x1_dram,
                              "biases": biases, "out": out})


def kernel(x, adj, L0_gnn_W_Q, L0_gnn_W_K, L0_gnn_W_V, L1_gnn_kernels, L1_gnn_attn_self, L1_gnn_attn_neigh,
           L1_gnn_biases):
    import concourse.bacc as bacc
    from concourse.bass_utils import run_bass_kernel_spmd

    def laid(a):
        return np.ascontiguousarray(np.asarray(a))

    arrays = {
        "x": laid(x), "adj": laid(adj), "adjT": laid(np.asarray(adj).T),
        "wqT": laid(np.asarray(L0_gnn_W_Q).T), "wkT": laid(np.asarray(L0_gnn_W_K).T), "wv": laid(L0_gnn_W_V),
        "wk1": laid(np.asarray(L1_gnn_kernels).transpose(1, 0, 2).reshape(D, HEADS * F)),
        "attn_self": laid(L1_gnn_attn_self).reshape(-1), "attn_neigh": laid(L1_gnn_attn_neigh).reshape(-1),
        "biases": laid(L1_gnn_biases).reshape(-1),
    }
    nc = bacc.Bacc("TRN2", target_bir_lowering=False, num_devices=1)
    args = [nc.dram_tensor(name, a.shape, F32, kind="ExternalInput").ap() for name, a in arrays.items()]
    out = nc.dram_tensor("out", (N, D), F32, kind="ExternalOutput").ap()
    program(nc, *args, out)
    result = run_bass_kernel_spmd(nc, [arrays], core_ids=[0])
    return result.results[0]["out"]
```

```python
from contextlib import ExitStack

import numpy as np
import concourse.bass as bass
from concourse import mybir

ALU = mybir.AluOpType
ACT = mybir.ActivationFunctionType
AX = mybir.AxisListType
F32 = mybir.dt.float32
F16 = mybir.dt.float16

P = 128
N, D = 4096, 512
HEADS, F = 8, 64
BLOCKS = N // P
DT = D // P
CHUNK = 512
CHUNKS = N // CHUNK
TPC = CHUNK // P
LN_EPS = 1e-5
SUM_EPS = float(np.finfo(np.float64).eps)
P_SCALE = 2.0 ** 15
G_TOP = 1024.0
G_LEAST = 1e-30
GROUPS = 2
GH = HEADS // GROUPS
MC = 1024
FX = GH * F + GH
QUERY, GRAPH = "query", "graph"


class RowBlock:

    def __init__(self, pair, offset):
        self.number = 2 * pair + offset
        self.parity = offset % 2
        self.pair = pair + offset // 2


def ge(eng, sem, value):
    if isinstance(value, int) and value <= 0:
        return
    eng.wait_ge(sem, value)


def hold(eng, held):
    eng.sem_inc(held, 1)


def pipeline(eng, step, lag):

    def static(j):
        step(lambda k: RowBlock(j // 2, j % 2 - k) if 0 <= j - k < BLOCKS else None)

    for j in range(4):
        static(j)
    with eng.Fori(2, BLOCKS // 2) as pair:
        for offset in range(2):
            step(lambda k: RowBlock(pair, offset - k))
    for j in range(BLOCKS, BLOCKS + lag):
        static(j)


def open_allocator(nc, stack, prefix):
    def sb(name, shape, dt=F32):
        return stack.enter_context(nc.sbuf_tensor(prefix + name, shape, dt))

    def ps(name, shape=(P, CHUNK)):
        return stack.enter_context(nc.psum_tensor(prefix + name, list(shape), F32))

    def sem(name):
        return stack.enter_context(nc.semaphore(prefix + name))

    return sb, ps, sem


def make_identity(nc, ident):
    with nc.semaphore("ident_zeroed") as zeroed, nc.semaphore("ident_done") as done, nc.Block() as block:

        @block.gpsimd
        def _(pool):
            pool.memset(ident[:, :], 0.0).then_inc(zeroed, 1)
            pool.wait_ge(zeroed, 1)
            pool.affine_select(out=ident[:, :], in_=ident[:, :], compare_op=ALU.not_equal, fill=1.0,
                               base=0, pattern=[[-1, P]], channel_multiplier=1).then_inc(done, 1)
            pool.wait_ge(done, 1)


def fold_query_key(nc, ident, wqT, wkT, m_sb):
    with ExitStack() as stack:
        sb, ps, sem = open_allocator(nc, stack, "m_")
        wq_sb = sb("wq", [P, DT, D])
        wk_sb = sb("wk", [P, DT, D])
        psM = ps("psM")
        loaded, product, copied = sem("loaded"), sem("product"), sem("copied")
        block = stack.enter_context(nc.Block())

        @block.sync
        def _(sp):
            sp.dma_start(wq_sb[:, :, :], wqT.rearrange("(t p) n -> p t n", p=P)).then_inc(loaded, 16)
            sp.dma_start(wk_sb[:, :, :], wkT.rearrange("(t p) n -> p t n", p=P)).then_inc(loaded, 16)

        @block.tensor
        def _(pe):
            pe.wait_ge(loaded, 32)
            for rows in range(DT):
                ge(pe, copied, rows)
                for t in range(DT):
                    mm = pe.matmul(psM[:, :], wq_sb[:, t, rows * P:(rows + 1) * P], wk_sb[:, t, :],
                                   start=(t == 0), stop=(t == DT - 1))
                mm.then_inc(product, 1)

        @block.scalar
        def _(act):
            for rows in range(DT):
                act.wait_ge(product, rows + 1)
                act.activation(m_sb[:, rows, :], psM[:, :], ACT.Copy).then_inc(copied, 1)
            act.wait_ge(copied, DT)


def project_rows(nc, kind, ident, rows, weights, res):
    query = kind == QUERY
    with ExitStack() as stack:
        sb, ps, sem = open_allocator(nc, stack, kind[0] + "_")
        xin = sb("xin", [P, 2, D])
        stats = sb("stats", [P, 6])
        mv = sb("mv", [P, 2])
        var = sb("var", [P, 1])
        std = sb("std", [P, 1])
        r0 = sb("r0", [P, 1])
        vrr = sb("vrr", [P, 1])
        corr = sb("corr", [P, 1])
        rstd = sb("rstd", [P, 2])
        shift = sb("shift", [P, 2])
        h = sb("h", [P, 2, D])
        hT = sb("hT", [P, 2, D])
        psT = [ps("psT0"), ps("psT1")]
        psY = [ps("psY0"), ps("psY1")]
        x_loaded = [sem("x_loaded0"), sem("x_loaded1")]
        w_loaded = sem("w_loaded")
        dve_stat = sem("dve_stat")
        var_ready, std_ready = sem("var_ready"), sem("std_ready")
        norm_ready, h_ready = sem("norm_ready"), sem("h_ready")
        hT_ready, hT_copied, y_ready = sem("hT_ready"), sem("hT_copied"), sem("y_ready")
        stored = [sem("stored0"), sem("stored1")]
        if query:
            gtop = sb("gtop", [P, 1])
            gunit = sb("gunit", [P, 1])
            ginv = sb("ginv", [P, 1])
            gs = sb("gs", [P, D])
            gT = sb("gT", [P, 2, 2, D], F16)
            psG = ps("psG")
            g_step = sem("g_step")
            gs_ready, gT_ready = sem("gs_ready"), sem("gT_ready")
            gT_high, gT_low = sem("gT_high"), sem("gT_low")
            hT_high, hT_low = sem("hT_high"), sem("hT_low")
            h_high, h_low = sem("h_high"), sem("h_low")
        else:
            asn = sb("asn", [P, 2, D])
            fx = sb("fx", [P, 2, GROUPS, FX])
            s_all = sb("s_all", [P, HEADS, BLOCKS])
            sT = sb("sT", [P, 2, P])
            prod = sb("prod", [P, 2, D])
            feats_copied, prod_ready, s_ready = sem("feats_copied"), sem("prod_ready"), sem("s_ready")
            record_ready = sem("record_ready")
            sT_ready, sT_copied, s_stored = sem("sT_ready"), sem("sT_copied"), sem("s_stored")
        held, held_store = sem("held"), sem("held_store")
        block = stack.enter_context(nc.Block())
        x_rows = rows.rearrange("(b p) d -> b p d", p=P)

        @block.sync
        def _(sp):
            if not query:
                sp.dma_start(weights, res["w_dram"].rearrange("(t p) n -> p t n", p=P)).then_inc(w_loaded, 16)
                for i, name in enumerate(("attn_self", "attn_neigh")):
                    sp.dma_start(asn[:, i, :], res[name].partition_broadcast(P)).then_inc(w_loaded, 16)

            def step(at):
                b = at(0)
                ge(sp, h_ready, b.number - 1)
                sp.dma_start(xin[:, b.parity, :], x_rows[b.number]).then_inc(x_loaded[b.parity], 16)

            pipeline(sp, step, 0)

        @block.scalar
        def _(act):
            def step(at):
                b, a, z = at(0), at(1), at(2)
                if b:
                    act.wait_ge(var_ready, b.number + 1)
                    act.activation(std[:, :], var[:, :], ACT.Sqrt).then_inc(std_ready, 1)
                if a:
                    act.wait_ge(hT_ready, a.number + 1)
                    ge(act, y_ready, a.number - 1)
                    if query:
                        ge(act, hT_low, a.number - 1)
                    act.activation(hT[:, a.parity, :], psT[a.parity][:, :], ACT.Copy).then_inc(hT_copied, 1)
                if z and not query:
                    act.wait_ge(y_ready, z.number + 1)
                    ge(act, stored[z.parity], 16 * z.pair)
                    act.activation(fx[:, z.parity, :, 0:GH * F],
                                   psY[z.parity][:, :].rearrange("p (g f) -> p g f", g=GROUPS),
                                   ACT.Copy).then_inc(feats_copied, 1)
                if b:
                    act.wait_ge(norm_ready, b.number + 1)
                    ge(act, hT_ready, b.number - 1)
                    if query:
                        ge(act, h_low, b.number - 1)
                    act.activation(h[:, b.parity, :], xin[:, b.parity, :], ACT.Relu,
                                   bias=shift[:, b.parity:b.parity + 1],
                                   scale=rstd[:, b.parity:b.parity + 1]).then_inc(h_ready, 1)
                if z and query:
                    act.wait_ge(gT_ready, z.number + 1)
                    ge(act, stored[z.parity], 16 * z.pair)
                    act.activation(gT[:, z.parity, 0, :], psG[:, :], ACT.Copy).then_inc(gT_high, 1)

            pipeline(act, step, 2)
            if not query:
                act.wait_ge(sT_ready, 2)
                for half in range(2):
                    act.activation(sT[:, half, :], psT[0][:, half * P:(half + 1) * P], ACT.Copy).then_inc(sT_copied, 1)

        @block.tensor
        def _(pe):
            ge(pe, w_loaded, 0 if query else 48)

            def step(at):
                a, z = at(1), at(2)
                if a:
                    pe.wait_ge(h_ready, a.number + 1)
                    ge(pe, hT_copied, a.number - 1)
                    for t in range(DT):
                        mm = pe.transpose(psT[a.parity][:, t * P:(t + 1) * P], h[:, a.parity, t * P:(t + 1) * P],
                                          ident[:, :])
                    mm.then_inc(hT_ready, 1)
                if z and query:
                    pe.wait_ge(gs_ready, z.number + 1)
                    ge(pe, gT_low, z.number)
                    for t in range(DT):
                        mm = pe.transpose(psG[:, t * P:(t + 1) * P], gs[:, t * P:(t + 1) * P], ident[:, :])
                    mm.then_inc(gT_ready, 1)
                if a:
                    pe.wait_ge(hT_copied, a.number + 1)
                    ge(pe, gs_ready if query else feats_copied, a.number - 1)
                    for t in range(DT):
                        mm = pe.matmul(psY[a.parity][:, :], hT[:, a.parity, t * P:(t + 1) * P], weights[:, t, :],
                                       start=(t == 0), stop=(t == DT - 1))
                    mm.then_inc(y_ready, 1)

            pipeline(pe, step, 2)
            if not query:
                pe.wait_ge(s_ready, BLOCKS)
                pe.wait_ge(hT_copied, BLOCKS)
                s_cols = s_all[:, :, :].rearrange("p h b -> p (h b)")
                for half in range(2):
                    pe.transpose(psT[0][:, half * P:(half + 1) * P], s_cols[:, half * P:(half + 1) * P],
                                 ident[:, :]).then_inc(sT_ready, 1)

        @block.gpsimd
        def _(pool):
            def step(at):
                a, z = at(1), at(2)
                if a and query:
                    pool.wait_ge(h_ready, a.number + 1)
                    pool.tensor_copy(res["h_hi"][:, a.number, :], h[:, a.parity, :]).then_inc(h_high, 1)
                    pool.wait_ge(h_high, a.number + 1)
                    pool.tensor_tensor(res["h_lo"][:, a.number, :], h[:, a.parity, :],
                                       res["h_hi"][:, a.number, :], ALU.subtract).then_inc(h_low, 1)
                if z and query:
                    pool.wait_ge(gT_low, z.number + 1)
                    pool.wait_ge(gT_high, z.number + 1)
                    hold(pool, held_store)
                    pool.dma_start(res["g_dram"][z.number], gT[:, z.parity, :, :]).then_inc(stored[z.parity], 16)
                if z and not query:
                    pool.wait_ge(feats_copied, z.number + 1)
                    pool.wait_ge(record_ready, z.number + 1)
                    hold(pool, held_store)
                    pool.dma_start(res["fx_dram"][z.number], fx[:, z.parity, :, :]).then_inc(stored[z.parity], 16)

            pipeline(pool, step, 2)
            if query:
                pool.wait_ge(h_low, BLOCKS)
            for s in stored:
                pool.wait_ge(s, 16 * BLOCKS // 2)
            if not query:
                pool.wait_ge(sT_copied, 2)
                pool.dma_start(res["s_dram"].rearrange("(i q) m -> q i m", i=2), sT[:, :, :]).then_inc(s_stored, 16)
                pool.wait_ge(s_stored, 16)

        @block.vector
        def _(dve):
            SMALL = 6

            def variance(b):
                n = b.number
                dve.wait_ge(x_loaded[b.parity], 16 * (b.pair + 1))
                dve.bn_stats(stats[:, :], xin[:, b.parity, :]).then_inc(dve_stat, 1)
                dve.wait_ge(dve_stat, SMALL * n + 1)
                hold(dve, held)
                dve.bn_aggr(mv[:, :], stats[:, :]).then_inc(dve_stat, 1)
                dve.wait_ge(dve_stat, SMALL * n + 2)
                dve.tensor_scalar(var[:, :], mv[:, 1:2], LN_EPS, None, ALU.add).then_inc(var_ready, 1)

            def norm(b):
                n = b.number
                dve.wait_ge(std_ready, n + 1)
                dve.reciprocal(r0[:, :], std[:, :]).then_inc(dve_stat, 1)
                dve.wait_ge(dve_stat, SMALL * n + 3)
                dve.scalar_tensor_tensor(out=vrr[:, :], in0=r0[:, :], scalar=var[:, :], in1=r0[:, :],
                                         op0=ALU.mult, op1=ALU.mult).then_inc(dve_stat, 1)
                dve.wait_ge(dve_stat, SMALL * n + 4)
                dve.tensor_scalar(corr[:, :], vrr[:, :], -0.5, 1.5, ALU.mult, ALU.add).then_inc(dve_stat, 1)
                dve.wait_ge(dve_stat, SMALL * n + 5)
                dve.tensor_tensor(rstd[:, b.parity:b.parity + 1], r0[:, :], corr[:, :], ALU.mult).then_inc(dve_stat, 1)
                dve.wait_ge(dve_stat, SMALL * n + 6)
                dve.scalar_tensor_tensor(out=shift[:, b.parity:b.parity + 1], in0=mv[:, 0:1], scalar=-1.0,
                                         in1=rstd[:, b.parity:b.parity + 1],
                                         op0=ALU.mult, op1=ALU.mult).then_inc(norm_ready, 1)

            def scale_g(z):
                n = z.number
                dve.wait_ge(y_ready, n + 1)
                ge(dve, gs_ready, n)
                dve.tensor_reduce(gtop[:, :], psY[z.parity][:, :], AX.X, ALU.max,
                                  apply_absolute_value=True).then_inc(g_step, 1)
                dve.wait_ge(g_step, 3 * n + 1)
                dve.tensor_scalar(gunit[:, :], gtop[:, :], G_LEAST, 1.0 / G_TOP, ALU.max, ALU.mult).then_inc(g_step, 1)
                dve.wait_ge(g_step, 3 * n + 2)
                dve.tensor_scalar(res["row_scale"][:, bass.ds(n, 1)], gunit[:, :], float(D) ** -0.5, None, ALU.mult)\
                   .then_inc(res["row_scale_ready"], 1)
                dve.reciprocal(ginv[:, :], gunit[:, :]).then_inc(g_step, 1)
                dve.wait_ge(g_step, 3 * n + 3)
                ge(dve, gT_ready, n)
                dve.tensor_scalar(gs[:, :], psY[z.parity][:, :], ginv[:, :], None, ALU.mult).then_inc(gs_ready, 1)

            def split_hT(a):
                n = a.number
                dve.wait_ge(hT_copied, n + 1)
                src = hT[:, a.parity, :].rearrange("p (t q) -> p t q", t=DT)
                dve.tensor_copy(res["hT_hi"][:, :, n, :], src).then_inc(hT_high, 1)
                dve.wait_ge(hT_high, n + 1)
                dve.tensor_tensor(res["hT_lo"][:, :, n, :], src, res["hT_hi"][:, :, n, :],
                                  ALU.subtract).then_inc(hT_low, 1)

            def split_g(z):
                dve.wait_ge(gT_high, z.number + 1)
                dve.tensor_tensor(gT[:, z.parity, 1, :], psG[:, :], gT[:, z.parity, 0, :],
                                  ALU.subtract).then_inc(gT_low, 1)

            def attention_terms(z):
                n = z.number
                if isinstance(n, int) and n == 0:
                    dve.wait_ge(w_loaded, 48)
                dve.wait_ge(feats_copied, n + 1)
                ge(dve, s_ready, n)
                ge(dve, record_ready, n)
                for i in range(2):
                    dve.tensor_tensor(prod[:, i, :].rearrange("p (g f) -> p g f", g=GROUPS),
                                      fx[:, z.parity, :, 0:GH * F],
                                      asn[:, i, :].rearrange("p (g f) -> p g f", g=GROUPS),
                                      ALU.mult).then_inc(prod_ready, 1)
                dve.wait_ge(prod_ready, 2 * n + 1)
                dve.tensor_reduce(s_all[:, :, n], prod[:, 0, :].rearrange("p (h f) -> p h f", h=HEADS),
                                  AX.X, ALU.add).then_inc(s_ready, 1)
                dve.wait_ge(prod_ready, 2 * n + 2)
                dve.tensor_reduce(fx[:, z.parity, :, GH * F:FX],
                                  prod[:, 1, :].rearrange("p (g h f) -> p g h f", g=GROUPS, h=GH),
                                  AX.X, ALU.add, negate=True).then_inc(record_ready, 1)

            def step(at):
                b, a, z = at(0), at(1), at(2)
                if b:
                    variance(b)
                if z and query:
                    scale_g(z)
                if b:
                    norm(b)
                if z and not query:
                    attention_terms(z)
                if a and query:
                    split_hT(a)
                if z and query:
                    split_g(z)

            pipeline(dve, step, 2)


def attend(nc, ident, res):
    with ExitStack() as stack:
        sb, ps, sem = open_allocator(nc, stack, "a_")
        wv = sb("wv", [P, DT, D])
        adj = sb("adj", [P, N])
        scores = sb("scores", [P, N])
        pT_hi = sb("pT_hi", [P, N], F16)
        pT_lo = sb("pT_lo", [P, N], F16)
        gT = sb("gT", [P, 2, 2, D], F16)
        row_scale = sb("row_scale", [P, 2])
        maxes = sb("maxes", [P, CHUNKS])
        neg_max = sb("neg_max", [P, 2])
        sums = sb("sums", [P, 2])
        recip = sb("recip", [P, 1])
        mean_h = sb("mean_h", [P, D])
        mean_hT = sb("mean_hT", [P, D])
        x_in = sb("x_in", [P, D])
        x1_out = sb("x1_out", [P, D])
        psS = [ps("psS0"), ps("psS1")]
        psT = [ps("psT0"), ps("psT1")]
        psU, psV, psY = ps("psU"), ps("psV"), ps("psY")
        wv_loaded, x_loaded, x1_stored = sem("wv_loaded"), sem("x_loaded"), sem("x1_stored")
        adj_loaded = [sem(f"adj_loaded{q}") for q in range(CHUNKS // 2)]
        g_loaded = [sem("g_loaded0"), sem("g_loaded1")]
        scale_ready = sem("scale_ready")
        scores_ready, scores_taken = sem("scores_ready"), sem("scores_taken")
        neg_ready, exp_ready = sem("neg_ready"), sem("exp_ready")
        pT_ready, pT_high, pT_low = sem("pT_ready"), sem("pT_high"), sem("pT_low")
        u_ready, recip_ready, mean_ready = sem("u_ready"), sem("recip_ready"), sem("mean_ready")
        meanT_ready, meanT_copied = sem("meanT_ready"), sem("meanT_copied")
        y_ready, x1_ready = sem("y_ready"), sem("x1_ready")
        held, held_store = sem("held"), sem("held_store")
        block = stack.enter_context(nc.Block())
        adj_rows = res["adj"].rearrange("(b p) m -> b p m", p=P)
        x_rows = res["x"].rearrange("(b p) d -> b p d", p=P)
        x1_rows = res["x1_dram"].rearrange("(b p) d -> b p d", p=P)

        @block.sync
        def _(sp):
            sp.dma_start(wv[:, :, :], res["w_v"].rearrange("(t p) n -> p t n", p=P)).then_inc(wv_loaded, 16)

            def step(at):
                b = at(0)
                ge(sp, scores_ready, CHUNKS * (b.number - 1))
                sp.dma_start(gT[:, b.parity, :, :], res["g_dram"][b.number]).then_inc(g_loaded[b.parity], 16)
                for q in range(CHUNKS // 2):
                    ge(sp, scores_taken, CHUNKS * (b.number - 1) + 2 * q + 2)
                    cols = slice(2 * q * CHUNK, (2 * q + 2) * CHUNK)
                    sp.dma_start(adj[:, cols], adj_rows[b.number, :, cols]).then_inc(adj_loaded[q], 16)

            pipeline(sp, step, 0)

        @block.gpsimd
        def _(pool):
            def step(at):
                a = at(2)
                if a:
                    ge(pool, x1_ready, a.number)
                    pool.wait_ge(mean_ready, a.number + 1)
                    hold(pool, held_store)
                    pool.dma_start(x_in[:, :], x_rows[a.number]).then_inc(x_loaded, 16)
                    pool.wait_ge(x1_ready, a.number + 1)
                    hold(pool, held_store)
                    pool.dma_start(x1_rows[a.number], x1_out[:, :]).then_inc(x1_stored, 16)

            pipeline(pool, step, 2)
            pool.wait_ge(x1_stored, 16 * BLOCKS)

        @block.tensor
        def _(pe):
            def transpose_p(a, c):
                if c == 0:
                    pe.wait_ge(exp_ready, a.number + 1)
                ge(pe, pT_low, CHUNKS * a.number + c - 1)
                for t in range(TPC):
                    col = c * CHUNK + t * P
                    mm = pe.transpose(psT[c % 2][:, t * P:(t + 1) * P], scores[:, col:col + P], ident[:, :])
                mm.then_inc(pT_ready, 1)

            def score(b, c):
                if c == 0:
                    pe.wait_ge(g_loaded[b.parity], 16 * (b.pair + 1))
                ge(pe, scores_taken, CHUNKS * b.number + c - 1)
                parts = [(g, t, hT) for t in range(DT) for g, hT in ((1, "hT_hi"), (0, "hT_lo"), (0, "hT_hi"))]
                for i, (g, t, hT) in enumerate(parts):
                    mm = pe.matmul(psS[c % 2][:, :], gT[:, b.parity, g, t * P:(t + 1) * P],
                                   res[hT][:, t, c * TPC:(c + 1) * TPC, :],
                                   start=(i == 0), stop=(i == len(parts) - 1))
                mm.then_inc(scores_ready, 1)

            def weighted_mean(a):
                ge(pe, mean_ready, a.number)
                for k in range(BLOCKS):
                    if k % TPC == 0:
                        pe.wait_ge(pT_low, CHUNKS * a.number + k // TPC + 1)
                    for i, (pT, h) in enumerate(((pT_lo, "h_hi"), (pT_hi, "h_lo"), (pT_hi, "h_hi"))):
                        mm = pe.matmul(psU[:, :], pT[:, k * P:(k + 1) * P], res[h][:, k, :],
                                       start=(k == 0 and i == 0), stop=(k == BLOCKS - 1 and i == 2))
                mm.then_inc(u_ready, 1)

            def step(at):
                b, a, z = at(0), at(1), at(2)
                for c in range(CHUNKS):
                    if a:
                        transpose_p(a, c)
                    if b:
                        score(b, c)
                    if z and c == 1:
                        pe.wait_ge(mean_ready, z.number + 1)
                        ge(pe, meanT_copied, z.number)
                        for t in range(DT):
                            mm = pe.transpose(psV[:, t * P:(t + 1) * P], mean_h[:, t * P:(t + 1) * P], ident[:, :])
                        mm.then_inc(meanT_ready, 1)
                    if z and c == 3:
                        if isinstance(z.number, int) and z.number == 0:
                            pe.wait_ge(wv_loaded, 16)
                        pe.wait_ge(meanT_copied, z.number + 1)
                        ge(pe, x1_ready, z.number)
                        for t in range(DT):
                            mm = pe.matmul(psY[:, :], mean_hT[:, t * P:(t + 1) * P], wv[:, t, :],
                                           start=(t == 0), stop=(t == DT - 1))
                        mm.then_inc(y_ready, 1)
                if a:
                    weighted_mean(a)

            pipeline(pe, step, 2)

        @block.scalar
        def _(act):
            def step(at):
                b, a, z = at(0), at(1), at(2)
                for c in range(CHUNKS):
                    if a:
                        act.wait_ge(pT_ready, CHUNKS * a.number + c + 1)
                        act.activation(pT_hi[:, c * CHUNK:(c + 1) * CHUNK], psT[c % 2][:, :], ACT.Copy,
                                       scale=P_SCALE).then_inc(pT_high, 1)
                    if z and c == 1:
                        act.wait_ge(meanT_ready, z.number + 1)
                        act.activation(mean_hT[:, :], psV[:, :], ACT.Copy).then_inc(meanT_copied, 1)
                if b:
                    act.wait_ge(neg_ready, b.number + 1)
                    act.activation(scores[:, :], scores[:, :], ACT.Exp, bias=neg_max[:, b.parity:b.parity + 1],
                                   accum_out=sums[:, b.parity:b.parity + 1]).then_inc(exp_ready, 1)

            pipeline(act, step, 2)

        @block.vector
        def _(dve):
            def step(at):
                b, a, z = at(0), at(1), at(2)
                if b:
                    ge(dve, scores_taken, CHUNKS * (b.number - 1))
                    dve.tensor_copy(row_scale[:, b.parity:b.parity + 1], res["row_scale"][:, bass.ds(b.number, 1)]
                                    ).then_inc(scale_ready, 1)
                    dve.wait_ge(scale_ready, b.number + 1)
                for c in range(CHUNKS):
                    cols = slice(c * CHUNK, (c + 1) * CHUNK)
                    if a:
                        dve.wait_ge(pT_high, CHUNKS * a.number + c + 1)
                        dve.scalar_tensor_tensor(out=pT_lo[:, cols], in0=psT[c % 2][:, :], scalar=P_SCALE,
                                                 in1=pT_hi[:, cols], op0=ALU.mult, op1=ALU.subtract
                                                 ).then_inc(pT_low, 1)
                    if b:
                        dve.wait_ge(adj_loaded[c // 2], 16 * (b.number + 1))
                        if c == 0:
                            ge(dve, neg_ready, b.number)
                        dve.wait_ge(scores_ready, CHUNKS * b.number + c + 1)
                        hold(dve, held)
                        dve.tensor_tensor_reduce(out=scores[:, cols], in0=psS[c % 2][:, :], in1=adj[:, cols],
                                                 scale=row_scale[:, b.parity:b.parity + 1], scalar=-3.0e38,
                                                 op0=ALU.mult, op1=ALU.max, accum_out=maxes[:, c:c + 1]
                                                 ).then_inc(scores_taken, 1)
                    if z and c == 3:
                        dve.wait_ge(y_ready, z.number + 1)
                        dve.wait_ge(x_loaded, 16 * (z.number + 1))
                        ge(dve, x1_stored, 16 * z.number)
                        dve.tensor_tensor(x1_out[:, :], psY[:, :], x_in[:, :], ALU.add).then_inc(x1_ready, 1)
                if b:
                    dve.wait_ge(scores_taken, CHUNKS * (b.number + 1))
                    dve.tensor_reduce(neg_max[:, b.parity:b.parity + 1], maxes[:, :], AX.X, ALU.max,
                                      negate=True).then_inc(neg_ready, 1)
                if a:
                    dve.wait_ge(exp_ready, a.number + 1)
                    dve.reciprocal(recip[:, :], sums[:, a.parity:a.parity + 1]).then_inc(recip_ready, 1)
                    dve.wait_ge(recip_ready, a.number + 1)
                    dve.wait_ge(u_ready, a.number + 1)
                    ge(dve, meanT_ready, a.number)
                    dve.tensor_scalar(mean_h[:, :], psU[:, :], recip[:, :], 1.0 / P_SCALE, ALU.mult, ALU.mult
                                      ).then_inc(mean_ready, 1)

            pipeline(dve, step, 2)


def aggregate(nc, ident, res):
    KS = 8
    AS = 4
    MT = MC // P
    HALVES = MC // CHUNK
    PAIRS = GH // 2
    ACT_HEADS = 2
    VEC_HEADS = GH - ACT_HEADS
    LEAD = 2
    FAR = 1e19
    with ExitStack() as stack:
        sb, ps, sem = open_allocator(nc, stack, "w_")
        far = sb("far", [P, AS, MC])
        fx = sb("fx", [P, KS, FX])
        s_rows = sb("s_rows", [P, 2, GH, MC])
        w = sb("w", [P, KS, GH, MC])
        zeros = sb("zeros", [P, P], F16)
        ones = sb("ones", [P, 32])
        bias = sb("bias", [P, HEADS * F])
        outT = sb("outT", [P, PAIRS + 1, MC])
        y = sb("y", [P, MT, GH * F])
        x1 = outT[:, 0:PAIRS, :].rearrange("p a m -> p (a m)").rearrange("p (t d) -> p t d", t=MT)
        recip = sb("recip", [P, MT, GH])
        psO = [[ps(f"psO{p}{half}") for half in range(HALVES)] for p in range(PAIRS)]
        psR = [ps(f"psR{half}") for half in range(HALVES)]
        psN = [ps("psN0"), ps("psN1")]
        adj_loaded = [sem(f"adj_loaded{i}") for i in range(AS)]
        fx_loaded = [sem(f"fx_loaded{i}") for i in range(KS)]
        s_loaded, bias_loaded, x1_loaded = sem("s_loaded"), sem("bias_loaded"), sem("x1_loaded")
        const_ready = sem("const_ready")
        far_ready, diff_ready = sem("far_ready"), sem("diff_ready")
        squared, pool_squared, exped, masked = sem("squared"), sem("pool_squared"), sem("exped"), sem("masked")
        w_used = sem("w_used")
        outT_copied, nat_ready, nat_taken = sem("outT_copied"), sem("nat_ready"), sem("nat_taken")
        eps_added, recip_ready, biased, y_ready = sem("eps_added"), sem("recip_ready"), sem("biased"), sem("y_ready")
        y_stored, held = sem("y_stored"), sem("held")
        block = stack.enter_context(nc.Block())
        adjT_view = res["adjT"].rearrange("(b p) (c m) -> b c p m", p=P, m=MC)
        s_view = res["s_dram"].rearrange("(g h b) m -> g h (b m)", g=GROUPS, h=GH)
        x1_view = res["x1_dram"].rearrange("(c t p) (g d) -> c g p t d", t=MT, p=P, g=GROUPS)
        y_view = res["out"].rearrange("(c t p) (g d) -> c g p t d", t=MT, p=P, g=GROUPS)

        BANKS = (PAIRS + 1) * HALVES
        PARTS = GROUPS * (N // MC)
        TURNS = BLOCKS // KS

        PIECE = 2
        PIECES = MT // PIECE
        ADD_AT = KS - PIECES - 1
        LOAD_AT = 3

        def nothing(*_):
            pass

        def sweep(eng, step, turn_tile=nothing, tile=nothing, first=nothing, late=nothing, last=nothing):
            def turn_of(o, c, group, turn, before=nothing, behind=nothing):
                for slot in range(KS):
                    u = TURNS * o + turn
                    before(slot)
                    step(o, c, group, KS * turn + slot, slot, u, KS * u + slot)
                    behind(slot)

            def part(c, group):
                o = GROUPS * c + group
                first(o, c, group)
                turn_of(o, c, group, 0)
                with eng.Fori(1, TURNS - 2) as turn:
                    turn_of(o, c, group, turn)
                if isinstance(o, int) and o == 0:
                    turn_of(o, c, group, TURNS - 2)
                    turn_of(o, c, group, TURNS - 1)
                else:
                    turn_of(o, c, group, TURNS - 2, lambda t: turn_tile(o - 1, t), lambda t: tile(o - 1, t))
                    turn_of(o, c, group, TURNS - 1, behind=lambda slot: late(o - 1, c - 1 + group, 1 - group, slot))
                    last(o - 1, c - 1 + group, 1 - group)

            part(0, 0)
            with eng.Fori(0, N // MC - 1) as c:
                part(c, 1)
                part(c + 1, 0)
            part(N // MC - 1, 1)

        @block.sync
        def _(sp):
            sp.dma_start(bias[:, :], res["biases"].partition_broadcast(P)).then_inc(bias_loaded, 16)

            def load_x1(q, c, group, slot=LOAD_AT):
                if slot != LOAD_AT:
                    return
                sp.wait_ge(nat_ready, MT * (q + 1))
                sp.dma_start(x1[:, :, :], x1_view[c, group]).then_inc(x1_loaded, 16)

            def first(o, c, group):
                if not (isinstance(o, int) and o < 2):
                    sp.wait_ge(w_used, KS + BLOCKS * (o - 1))
                sp.dma_start(s_rows[:, group, :, :],
                             s_view[group, :, bass.ds(c * MC, MC)].partition_broadcast(P)).then_inc(s_loaded, 16)

            def step(o, c, group, k, slot, u, g):
                sp.wait_ge(masked, g + 1)
                hold(sp, held)
                sp.dma_start(far[:, slot % AS, :], adjT_view[k, c]).then_inc(adj_loaded[slot % AS], 16)
                sp.wait_ge(w_used, g + 1)
                sp.dma_start(fx[:, slot, :], res["fx_dram"][k, :, group, :]).then_inc(fx_loaded[slot], 16)

            sweep(sp, step, first=first, late=load_x1)
            load_x1(PARTS - 1, N // MC - 1, 1)

        @block.scalar
        def _(act):
            def step(o, c, group, k, slot, u, g):
                act.wait_ge(s_loaded, 16 * (o + 1))
                act.wait_ge(fx_loaded[slot], 16 * (u + 1))
                act.wait_ge(w_used, g + 1)
                for a in range(ACT_HEADS):
                    act.activation(w[:, slot, a, :], s_rows[:, group, a, :], ACT.Square,
                                   bias=fx[:, slot, GH * F + a:GH * F + a + 1]).then_inc(squared, 1)
                act.wait_ge(squared, ACT_HEADS * (g + 1))
                act.wait_ge(pool_squared, g + 1)
                act.activation(w[:, slot, :, :], w[:, slot, :, :], ACT.Exp, scale=-1.0).then_inc(exped, 1)

            def store_y(q, c, group):
                act.wait_ge(y_ready, 1 + PIECES * (q + 1))
                act.dma_start(y_view[c, group], y[:, :, :]).then_inc(y_stored, 16)

            sweep(act, step, last=store_y)
            store_y(PARTS - 1, N // MC - 1, 1)
            act.wait_ge(y_stored, 16 * (PARTS + 1))

        @block.gpsimd
        def _(pool):
            pool.sem_inc(w_used, KS)
            pool.sem_inc(masked, AS)
            pool.sem_inc(nat_taken, 2)
            pool.sem_inc(y_stored, 16)
            pool.sem_inc(y_ready, 1)
            pool.memset(zeros[:, :], 0.0).then_inc(const_ready, 1)
            pool.memset(ones[:, :], 1.0).then_inc(const_ready, 1)

            def step(o, c, group, k, slot, u, g):
                pool.wait_ge(diff_ready, VEC_HEADS * (g + 1))
                half = w[:, slot, ACT_HEADS:GH, :]
                pool.tensor_tensor(half, half, half, ALU.mult).then_inc(pool_squared, 1)

            def add_bias(q, c, group, slot):
                if slot >= PIECES:
                    return
                n = PIECES * q + slot + 1
                pool.wait_ge(nat_taken, 2 + PIECE * n)
                columns = bias[:, group * GH * F:(group + 1) * GH * F]
                piece = y[:, PIECE * slot:PIECE * (slot + 1), :]
                pool.tensor_tensor(piece, piece, columns.unsqueeze(1).broadcast_to([P, PIECE, GH * F]),
                                   ALU.add).then_inc(biased, 1)

            pool.wait_ge(bias_loaded, 16)
            sweep(pool, step, late=add_bias)
            for slot in range(PIECES):
                add_bias(PARTS - 1, N // MC - 1, 1, slot)

        @block.vector
        def _(dve):
            def differ(o, group, slot, u, g):
                dve.wait_ge(s_loaded, 16 * (o + 1))
                dve.wait_ge(adj_loaded[slot % AS], 16 * (KS // AS * u + slot // AS + 1))
                here = far[:, slot % AS, :]
                dve.tensor_scalar(here, here, 0.0, FAR, ALU.is_le, ALU.mult).then_inc(far_ready, 1)
                dve.wait_ge(fx_loaded[slot], 16 * (u + 1))
                dve.wait_ge(w_used, g + 1)
                dve.wait_ge(far_ready, g + 1)
                for a in range(ACT_HEADS, GH):
                    dve.scalar_tensor_tensor(out=w[:, slot, a, :], in0=s_rows[:, group, a, :],
                                             scalar=fx[:, slot, GH * F + a:GH * F + a + 1], in1=here,
                                             op0=ALU.add, op1=ALU.add).then_inc(diff_ready, 1)

            def mask(slot, g):
                dve.wait_ge(exped, g + 1)
                dve.scalar_tensor_tensor(out=w[:, slot, 0:ACT_HEADS, :],
                                         in0=far[:, slot % AS, :].unsqueeze(1).broadcast_to([P, ACT_HEADS, MC]),
                                         scalar=0.0, in1=w[:, slot, 0:ACT_HEADS, :],
                                         op0=ALU.is_equal, op1=ALU.mult).then_inc(masked, 1)

            def step(o, c, group, k, slot, u, g):
                ahead = (slot + LEAD) % KS, u + (slot + LEAD) // KS, g + LEAD
                if not (isinstance(k, int) and k + LEAD >= BLOCKS):
                    differ(o, group, *ahead)
                elif not (isinstance(o, int) and o == PARTS - 1):
                    differ(o + 1, 1 - group, *ahead)
                if isinstance(k, int) and k == 0 and not (isinstance(o, int) and o == 0):
                    copy_out(o - 1)
                mask(slot, g)

            def copy_out(q):
                dve.wait_ge(w_used, KS + BLOCKS * (q + 1))
                dve.wait_ge(y_ready, 1 + PIECES * q)
                for i, banks in enumerate(psO + [psR]):
                    for half in range(HALVES):
                        dve.tensor_copy(outT[:, i, half * CHUNK:(half + 1) * CHUNK], banks[half][:, :]
                                        ).then_inc(outT_copied, 1)

            def normalise(q, t):
                if t == 0:
                    dve.wait_ge(y_stored, 16 * (q + 1))
                nat = psN[t % 2]
                n = MT * q + t
                dve.wait_ge(nat_ready, n + 1)
                sums = nat[:, PAIRS * P:(PAIRS + 1) * P].rearrange("p (a r) -> p a r", a=GH)[:, :, 0]
                dve.tensor_scalar(recip[:, t, :], sums, SUM_EPS, None, ALU.add).then_inc(eps_added, 1)
                dve.wait_ge(eps_added, n + 1)
                dve.reciprocal(recip[:, t, :], recip[:, t, :]).then_inc(recip_ready, 1)
                dve.wait_ge(recip_ready, n + 1)
                dve.tensor_tensor(y[:, t, :].rearrange("p (a f) -> p a f", a=GH),
                                  nat[:, 0:PAIRS * P].rearrange("p (a f) -> p a f", a=GH),
                                  recip[:, t, :].unsqueeze(2).broadcast_to([P, GH, F]), ALU.mult
                                  ).then_inc(nat_taken, 1)

            def add_x1(q, c, group, slot):
                i = slot - ADD_AT
                if not 0 <= i < PIECES:
                    return
                if i == 0:
                    dve.wait_ge(x1_loaded, 16 * (q + 1))
                n = PIECES * q + i + 1
                dve.wait_ge(biased, n)
                piece = y[:, PIECE * i:PIECE * (i + 1), :]
                dve.scalar_tensor_tensor(out=piece, in0=piece, scalar=0.0, in1=x1[:, PIECE * i:PIECE * (i + 1), :],
                                         op0=ALU.max, op1=ALU.add).then_inc(y_ready, 1)

            def first(o, c, group):
                if isinstance(o, int) and o == 0:
                    for slot in range(LEAD):
                        differ(o, group, slot, 0, slot)

            sweep(dve, step, tile=normalise, first=first, late=add_x1)
            copy_out(PARTS - 1)
            for t in range(MT):
                normalise(PARTS - 1, t)
            for i in range(PIECES):
                add_x1(PARTS - 1, N // MC - 1, 1, ADD_AT + i)

        @block.tensor
        def _(pe):
            pe.wait_ge(const_ready, 2)

            def first(o, c, group):
                ge(pe, outT_copied, BANKS * o)
                for bank in psO[0] + psO[1] + psR:
                    pe.matmul(bank[:, :].rearrange("p (i q) -> p i q", q=P), zeros[:, :],
                              zeros[:, :].unsqueeze(1).broadcast_to([P, CHUNK // P, P]), start=True, stop=False, skip_group_check=True)

            def step(o, c, group, k, slot, u, g):
                for pair in reversed(range(PAIRS)):
                    if pair:
                        pe.wait_ge(exped, g + 1)
                    else:
                        pe.wait_ge(masked, AS + g + 1)
                    for half in range(HALVES):
                        for i in range(2):
                            a = 2 * pair + i
                            pe.matmul(psO[pair][half][F * i:F * i + F, :], fx[:, slot, F * a:F * a + F],
                                      w[:, slot, a, half * CHUNK:(half + 1) * CHUNK],
                                      start=False, stop=False, skip_group_check=True)
                for half in range(HALVES):
                    for a in range(GH):
                        mm = pe.matmul(psR[half][32 * a:32 * a + 32, :], ones[:, :],
                                       w[:, slot, a, half * CHUNK:(half + 1) * CHUNK],
                                       start=False, stop=False, skip_group_check=True)
                mm.then_inc(w_used, 1)

            def turn_back(q, t):
                if t == 0:
                    pe.wait_ge(outT_copied, BANKS * (q + 1))
                pe.wait_ge(nat_taken, MT * q + t + 1)
                for i in range(PAIRS + 1):
                    mm = pe.transpose(psN[t % 2][:, i * P:(i + 1) * P], outT[:, i, t * P:(t + 1) * P], ident[:, :])
                mm.then_inc(nat_ready, 1)

            sweep(pe, step, turn_tile=turn_back, first=first)
            for t in range(MT):
                turn_back(PARTS - 1, t)


def program(nc, x, adj, adjT, wqT, wkT, wv, wk1, attn_self, attn_neigh, biases, out):
    g_dram = nc.dram_tensor("g_dram", [BLOCKS, P, 2, D], F16).ap()
    x1_dram = nc.dram_tensor("x1_dram", [N, D], F32).ap()
    fx_dram = nc.dram_tensor("fx_dram", [BLOCKS, P, GROUPS, FX], F32).ap()
    s_dram = nc.dram_tensor("s_dram", [HEADS * BLOCKS, P], F32).ap()
    with nc.sbuf_tensor("ident", [P, P], F32) as ident:
        make_identity(nc, ident)
        with ExitStack() as stack:
            def resident(name, shape, dt):
                return stack.enter_context(nc.sbuf_tensor(name, shape, dt))

            res = {"x": x, "adj": adj, "w_v": wv, "g_dram": g_dram, "x1_dram": x1_dram,
                   "h_hi": resident("h_hi", [P, BLOCKS, D], F16), "h_lo": resident("h_lo", [P, BLOCKS, D], F16),
                   "hT_hi": resident("hT_hi", [P, DT, BLOCKS, P], F16),
                   "hT_lo": resident("hT_lo", [P, DT, BLOCKS, P], F16),
                   "row_scale": resident("row_scales", [P, BLOCKS], F32)}
            with nc.sbuf_tensor("m_sb", [P, DT, D], F32) as m_sb, nc.semaphore("row_scale_ready") as ready:
                fold_query_key(nc, ident, wqT, wkT, m_sb)
                res["row_scale_ready"] = ready
                project_rows(nc, QUERY, ident, x, m_sb, res)
            attend(nc, ident, res)
        with nc.sbuf_tensor("wk1_sb", [P, DT, D], F32) as wk1_sb:
            project_rows(nc, GRAPH, ident, x1_dram, wk1_sb[:, :, :],
                         {"w_dram": wk1, "attn_self": attn_self, "attn_neigh": attn_neigh,
                          "fx_dram": fx_dram, "s_dram": s_dram})
        aggregate(nc, ident, {"adjT": adjT, "fx_dram": fx_dram, "s_dram": s_dram, "x1_dram": x1_dram,
                              "biases": biases, "out": out})


def kernel(x, adj, L0_gnn_W_Q, L0_gnn_W_K, L0_gnn_W_V, L1_gnn_kernels, L1_gnn_attn_self, L1_gnn_attn_neigh,
           L1_gnn_biases):
    import concourse.bacc as bacc
    from concourse.bass_utils import run_bass_kernel_spmd

    def laid(a):
        return np.ascontiguousarray(np.asarray(a))

    arrays = {
        "x": laid(x), "adj": laid(adj), "adjT": laid(np.asarray(adj).T),
        "wqT": laid(np.asarray(L0_gnn_W_Q).T), "wkT": laid(np.asarray(L0_gnn_W_K).T), "wv": laid(L0_gnn_W_V),
        "wk1": laid(np.asarray(L1_gnn_kernels).transpose(1, 0, 2).reshape(D, HEADS * F)),
        "attn_self": laid(L1_gnn_attn_self).reshape(-1), "attn_neigh": laid(L1_gnn_attn_neigh).reshape(-1),
        "biases": laid(L1_gnn_biases).reshape(-1),
    }
    nc = bacc.Bacc("TRN2", target_bir_lowering=False, num_devices=1)
    args = [nc.dram_tensor(name, a.shape, F32, kind="ExternalInput").ap() for name, a in arrays.items()]
    out = nc.dram_tensor("out", (N, D), F32, kind="ExternalOutput").ap()
    program(nc, *args, out)
    result = run_bass_kernel_spmd(nc, [arrays], core_ids=[0])
    return result.results[0]["out"]
```

```python
from contextlib import ExitStack

import numpy as np
import concourse.bass as bass
from concourse import mybir

ALU = mybir.AluOpType
ACT = mybir.ActivationFunctionType
AX = mybir.AxisListType
F32 = mybir.dt.float32
F16 = mybir.dt.float16

P = 128
N, D = 4096, 512
HEADS, F = 8, 64
BLOCKS = N // P
DT = D // P
CHUNK = 512
CHUNKS = N // CHUNK
TPC = CHUNK // P
LN_EPS = 1e-5
SUM_EPS = float(np.finfo(np.float64).eps)
P_SCALE = 2.0 ** 15
G_TOP = 1024.0
LEAST = 1e-30
M_TOP = 1024.0
W_TOP = 64.0
GROUPS = 2
GH = HEADS // GROUPS
MC = 1024
FX = GH * F + GH
QUERY, GRAPH = "query", "graph"


class RowBlock:

    def __init__(self, pair, offset):
        self.number = 2 * pair + offset
        self.parity = offset % 2
        self.pair = pair + offset // 2


def ge(eng, sem, value):
    if isinstance(value, int) and value <= 0:
        return
    eng.wait_ge(sem, value)


def hold(eng, held):
    eng.sem_inc(held, 1)


def pipeline(eng, step, lag):

    def static(j):
        step(lambda k: RowBlock(j // 2, j % 2 - k) if 0 <= j - k < BLOCKS else None)

    for j in range(4):
        static(j)
    with eng.Fori(2, BLOCKS // 2) as pair:
        for offset in range(2):
            step(lambda k: RowBlock(pair, offset - k))
    for j in range(BLOCKS, BLOCKS + lag):
        static(j)


def open_allocator(nc, stack, prefix):
    def sb(name, shape, dt=F32):
        return stack.enter_context(nc.sbuf_tensor(prefix + name, shape, dt))

    def ps(name, shape=(P, CHUNK)):
        return stack.enter_context(nc.psum_tensor(prefix + name, list(shape), F32))

    def sem(name):
        return stack.enter_context(nc.semaphore(prefix + name))

    return sb, ps, sem


def make_identity(nc, ident):
    with nc.semaphore("ident_zeroed") as zeroed, nc.semaphore("ident_done") as done, nc.Block() as block:

        @block.gpsimd
        def _(pool):
            pool.memset(ident[:, :], 0.0).then_inc(zeroed, 1)
            pool.wait_ge(zeroed, 1)
            pool.affine_select(out=ident[:, :], in_=ident[:, :], compare_op=ALU.not_equal, fill=1.0,
                               base=0, pattern=[[-1, P]], channel_multiplier=1).then_inc(done, 1)
            pool.wait_ge(done, 1)


def prepare_weights(nc, ident, wqT, wkT, wv, wvT, m_parts, v_parts, m_unit, v_unit):
    with ExitStack() as stack:
        sb, ps, sem = open_allocator(nc, stack, "m_")
        wq_sb = sb("wq", [P, DT, D])
        wk_sb = sb("wk", [P, DT, D])
        wvT_sb = sb("wvT", [P, DT, D])
        wv_sb = sb("wv", [P, DT, D])
        m_sb = sb("m", [P, DT, D])
        m_top = sb("m_top", [P, 1])
        m_diagonal = sb("m_diagonal", [P, P])
        m_inverse = sb("m_inverse", [P, 1])
        top = sb("top", [P, DT])
        unit = sb("unit", [P, DT])
        diagonal = sb("diagonal", [P, DT, P])
        ones = sb("ones", [P, P])
        scale = sb("scale", [P, D])
        psM, psW, psTop = [ps("psM0"), ps("psM1")], ps("psW"), ps("psTop")
        m_step, m_spread, parts_step = sem("m_step"), sem("m_spread"), sem("parts_step")
        loaded, product, copied = sem("loaded"), sem("product"), sem("copied")
        wv_loaded, ones_ready = sem("wv_loaded"), sem("ones_ready")
        top_ready, unit_ready, diagonal_ready = sem("top_ready"), sem("unit_ready"), sem("diagonal_ready")
        spread, scale_ready = sem("spread"), sem("scale_ready")
        wv_scaled, v_unit_ready = sem("wv_scaled"), sem("v_unit_ready")
        block = stack.enter_context(nc.Block())

        @block.sync
        def _(sp):
            sp.dma_start(wq_sb[:, :, :], wqT.rearrange("(t p) n -> p t n", p=P)).then_inc(loaded, 16)
            sp.dma_start(wk_sb[:, :, :], wkT.rearrange("(t p) n -> p t n", p=P)).then_inc(loaded, 16)
            sp.dma_start(wvT_sb[:, :, :], wvT.rearrange("(t p) n -> p t n", p=P)).then_inc(wv_loaded, 16)
            sp.dma_start(wv_sb[:, :, :], wv.rearrange("(t p) n -> p t n", p=P)).then_inc(wv_loaded, 16)

        @block.gpsimd
        def _(pool):
            pool.memset(ones[:, :], 1.0).then_inc(ones_ready, 1)

        @block.tensor
        def _(pe):
            pe.wait_ge(loaded, 32)
            for rows in range(DT):
                ge(pe, copied, rows - 1)
                for t in range(DT):
                    mm = pe.matmul(psM[rows % 2][:, :], wq_sb[:, t, rows * P:(rows + 1) * P], wk_sb[:, t, :],
                                   start=(t == 0), stop=(t == DT - 1))
                mm.then_inc(product, 1)
            pe.wait_ge(ones_ready, 1)
            pe.wait_ge(diagonal_ready, DT)
            for t in range(DT):
                mm = pe.matmul(psW[:, t * P:(t + 1) * P], ones[:, :], diagonal[:, t, :], start=True, stop=True)
            mm.then_inc(spread, 1)
            pe.wait_ge(m_step, 2)
            pe.matmul(psTop[:, 0:P], ones[:, :], m_diagonal[:, :], start=True, stop=True).then_inc(m_spread, 1)

        @block.scalar
        def _(act):
            for rows in range(DT):
                act.wait_ge(product, rows + 1)
                act.activation(m_sb[:, rows, :], psM[rows % 2][:, :], ACT.Copy).then_inc(copied, 1)
            act.wait_ge(copied, DT)

        @block.vector
        def _(dve):
            dve.wait_ge(wv_loaded, 32)
            dve.tensor_reduce(top[:, :], wvT_sb[:, :, :], AX.X, ALU.max, apply_absolute_value=True
                              ).then_inc(top_ready, 1)
            dve.wait_ge(top_ready, 1)
            dve.tensor_scalar(unit[:, :], top[:, :], LEAST, 1.0 / W_TOP, ALU.max, ALU.mult).then_inc(unit_ready, 1)
            dve.wait_ge(unit_ready, 1)
            for t in range(DT):
                dve.tensor_scalar(diagonal[:, t, :], ident[:, :], unit[:, t:t + 1], None, ALU.mult
                                  ).then_inc(diagonal_ready, 1)
            dve.wait_ge(spread, 1)
            dve.reciprocal(scale[:, :], psW[:, :]).then_inc(scale_ready, 1)
            dve.tensor_scalar(v_unit[:, :], psW[:, :], 1.0 / P_SCALE, None, ALU.mult).then_inc(v_unit_ready, 1)
            dve.wait_ge(scale_ready, 1)
            dve.tensor_tensor(wv_sb[:, :, :], wv_sb[:, :, :], scale[:, :].unsqueeze(1).broadcast_to([P, DT, D]),
                              ALU.mult).then_inc(wv_scaled, 1)
            dve.wait_ge(wv_scaled, 1)
            dve.tensor_copy(v_parts[:, 0, :, :], wv_sb[:, :, :]).then_inc(parts_step, 1)
            dve.wait_ge(parts_step, 1)
            dve.tensor_tensor(v_parts[:, 1, :, :], wv_sb[:, :, :], v_parts[:, 0, :, :], ALU.subtract
                              ).then_inc(parts_step, 1)
            dve.wait_ge(copied, DT)
            dve.tensor_reduce(m_top[:, :], m_sb[:, :, :].rearrange("p t n -> p (t n)"), AX.X, ALU.max,
                              apply_absolute_value=True).then_inc(m_step, 1)
            dve.wait_ge(m_step, 1)
            dve.tensor_scalar(m_diagonal[:, :], ident[:, :], m_top[:, :], None, ALU.mult).then_inc(m_step, 1)
            dve.wait_ge(m_spread, 1)
            dve.tensor_reduce(m_top[:, :], psTop[:, 0:P], AX.X, ALU.max, apply_absolute_value=True
                              ).then_inc(m_step, 1)
            dve.wait_ge(m_step, 3)
            dve.tensor_scalar(m_top[:, :], m_top[:, :], LEAST, 1.0 / M_TOP, ALU.max, ALU.mult).then_inc(m_step, 1)
            dve.wait_ge(m_step, 4)
            dve.tensor_scalar(m_unit[:, :], m_top[:, :], float(D) ** -0.5, None, ALU.mult).then_inc(m_step, 1)
            dve.reciprocal(m_inverse[:, :], m_top[:, :]).then_inc(m_step, 1)
            dve.wait_ge(m_step, 6)
            dve.tensor_scalar(m_parts[:, 0, :, :], m_sb[:, :, :], m_inverse[:, :], None, ALU.mult
                              ).then_inc(parts_step, 1)
            dve.wait_ge(parts_step, 3)
            dve.scalar_tensor_tensor(out=m_parts[:, 1, :, :], in0=m_sb[:, :, :], scalar=m_inverse[:, :],
                                     in1=m_parts[:, 0, :, :], op0=ALU.mult, op1=ALU.subtract
                                     ).then_inc(parts_step, 1)
            dve.wait_ge(v_unit_ready, 1)
            dve.wait_ge(parts_step, 4)


def project_rows(nc, kind, ident, rows, weights, res):
    query = kind == QUERY
    with ExitStack() as stack:
        sb, ps, sem = open_allocator(nc, stack, kind[0] + "_")
        xin = sb("xin", [P, 2, D])
        stats = sb("stats", [P, 6])
        mv = sb("mv", [P, 2])
        var = sb("var", [P, 1])
        std = sb("std", [P, 1])
        r0 = sb("r0", [P, 1])
        vrr = sb("vrr", [P, 1])
        corr = sb("corr", [P, 1])
        rstd = sb("rstd", [P, 2])
        shift = sb("shift", [P, 2])
        h = sb("h", [P, 2, D])
        psT = [ps("psT0"), ps("psT1")]
        psY = [ps("psY0"), ps("psY1")]
        x_loaded = [sem("x_loaded0"), sem("x_loaded1")]
        w_loaded = sem("w_loaded")
        dve_stat = sem("dve_stat")
        var_ready, std_ready = sem("var_ready"), sem("std_ready")
        norm_ready, h_ready = sem("norm_ready"), sem("h_ready")
        hT_ready, hT_copied, y_ready = sem("hT_ready"), sem("hT_copied"), sem("y_ready")
        stored = [sem("stored0"), sem("stored1")]
        if query:
            gtop = sb("gtop", [P, 1])
            gunit = sb("gunit", [P, 1])
            ginv = sb("ginv", [P, 1])
            gs = sb("gs", [P, D])
            gT = sb("gT", [P, 2, 2, D], F16)
            hT = sb("hT", [P, 2, 2, D], F16)
            hT_kept = sem("hT_kept")
            psG = ps("psG")
            psV = [ps("psV0"), ps("psV1")]
            v_ready, v_high, v_low = sem("v_ready"), sem("v_high"), sem("v_low")
            held_v = sem("held_v")
            g_step = sem("g_step")
            gs_ready, gT_ready = sem("gs_ready"), sem("gT_ready")
            gT_high, gT_low = sem("gT_high"), sem("gT_low")
            hT_high, hT_low = sem("hT_high"), sem("hT_low")
        else:
            hT = sb("hT", [P, 2, D])
            asn = sb("asn", [P, 2, D])
            fx = sb("fx", [P, 2, GROUPS, FX])
            s_all = sb("s_all", [P, HEADS, BLOCKS])
            sT = sb("sT", [P, 2, P])
            prod = sb("prod", [P, 2, D])
            self_prod_ready, neigh_prod_ready = sem("self_prod_ready"), sem("neigh_prod_ready")
            feats_copied, s_ready, record_ready = sem("feats_copied"), sem("s_ready"), sem("record_ready")
            sT_ready, sT_copied, s_stored = sem("sT_ready"), sem("sT_copied"), sem("s_stored")
        held, held_store = sem("held"), sem("held_store")
        block = stack.enter_context(nc.Block())
        x_rows = rows.rearrange("(b p) d -> b p d", p=P)

        @block.sync
        def _(sp):
            if not query:
                sp.dma_start(weights, res["w_dram"].rearrange("(t p) n -> p t n", p=P)).then_inc(w_loaded, 16)
                for i, name in enumerate(("attn_self", "attn_neigh")):
                    sp.dma_start(asn[:, i, :], res[name].partition_broadcast(P)).then_inc(w_loaded, 16)

            def step(at):
                b = at(0)
                ge(sp, h_ready, b.number - 1)
                sp.dma_start(xin[:, b.parity, :], x_rows[b.number]).then_inc(x_loaded[b.parity], 16)

            pipeline(sp, step, 0)

        @block.scalar
        def _(act):
            def step(at):
                b, a, z = at(0), at(1), at(2)
                if b:
                    act.wait_ge(var_ready, b.number + 1)
                    act.activation(std[:, :], var[:, :], ACT.Sqrt).then_inc(std_ready, 1)
                if a:
                    act.wait_ge(hT_ready, a.number + 1)
                    ge(act, v_ready if query else y_ready, a.number - 1)
                    if query:
                        ge(act, hT_kept, 2 * (a.number - 1))
                        act.activation(hT[:, a.parity, 0, :], psT[a.parity][:, :], ACT.Copy).then_inc(hT_high, 1)
                    else:
                        act.activation(hT[:, a.parity, :], psT[a.parity][:, :], ACT.Copy).then_inc(hT_copied, 1)
                if z and query:
                    act.wait_ge(v_ready, z.number + 1)
                    hold(act, held_v)
                    act.activation(res["v_hi"][:, z.number, :], psV[z.parity][:, :], ACT.Copy).then_inc(v_high, 1)
                if z and not query:
                    act.wait_ge(y_ready, z.number + 1)
                    ge(act, stored[z.parity], 16 * z.pair)
                    act.activation(fx[:, z.parity, :, 0:GH * F],
                                   psY[z.parity][:, :].rearrange("p (g f) -> p g f", g=GROUPS),
                                   ACT.Copy).then_inc(feats_copied, 1)
                if b:
                    act.wait_ge(norm_ready, b.number + 1)
                    ge(act, hT_ready, b.number - 1)
                    act.activation(h[:, b.parity, :], xin[:, b.parity, :], ACT.Relu,
                                   bias=shift[:, b.parity:b.parity + 1],
                                   scale=rstd[:, b.parity:b.parity + 1]).then_inc(h_ready, 1)
                if z and query:
                    act.wait_ge(gT_ready, z.number + 1)
                    ge(act, stored[z.parity], 16 * z.pair)
                    act.activation(gT[:, z.parity, 0, :], psG[:, :], ACT.Copy).then_inc(gT_high, 1)

            pipeline(act, step, 2)
            if not query:
                act.wait_ge(sT_ready, 2)
                for half in range(2):
                    act.activation(sT[:, half, :], psT[0][:, half * P:(half + 1) * P], ACT.Copy).then_inc(sT_copied, 1)
                act.wait_ge(sT_copied, 2)
                act.dma_start(res["s_dram"].rearrange("(i q) m -> q i m", i=2), sT[:, :, :]).then_inc(s_stored, 16)
                act.wait_ge(s_stored, 16)

        @block.tensor
        def _(pe):
            ge(pe, w_loaded, 0 if query else 48)

            def product(ps, row, parts, ready):
                passes = ((0, 0), (0, 1), (1, 0))
                for i, (h_part, w_part) in enumerate(passes):
                    if i == 0:
                        pe.wait_ge(hT_high, row.number + 1)
                    if i == 2:
                        pe.wait_ge(hT_low, row.number + 1)
                    for t in range(DT):
                        mm = pe.matmul(ps[row.parity][:, :], hT[:, row.parity, h_part, t * P:(t + 1) * P],
                                       parts[:, w_part, t, :], start=(i == 0 and t == 0),
                                       stop=(i == len(passes) - 1 and t == DT - 1))
                mm.then_inc(ready, 1)

            def step(at):
                a, z = at(1), at(2)
                if a:
                    pe.wait_ge(h_ready, a.number + 1)
                    ge(pe, hT_low if query else hT_copied, a.number - 1)
                    for t in range(DT):
                        mm = pe.transpose(psT[a.parity][:, t * P:(t + 1) * P], h[:, a.parity, t * P:(t + 1) * P],
                                          ident[:, :])
                    mm.then_inc(hT_ready, 1)
                if z and query:
                    ge(pe, v_low, z.number - 1)
                    product(psV, z, res["v_parts"], v_ready)
                    pe.wait_ge(gs_ready, z.number + 1)
                    ge(pe, gT_low, z.number)
                    for t in range(DT):
                        mm = pe.transpose(psG[:, t * P:(t + 1) * P], gs[:, t * P:(t + 1) * P], ident[:, :])
                    mm.then_inc(gT_ready, 1)
                if a and query:
                    ge(pe, gs_ready, a.number - 1)
                    product(psY, a, weights, y_ready)
                if a and not query:
                    pe.wait_ge(hT_copied, a.number + 1)
                    ge(pe, feats_copied, a.number - 1)
                    for t in range(DT):
                        mm = pe.matmul(psY[a.parity][:, :], hT[:, a.parity, t * P:(t + 1) * P], weights[:, t, :],
                                       start=(t == 0), stop=(t == DT - 1))
                    mm.then_inc(y_ready, 1)

            pipeline(pe, step, 2)
            if not query:
                pe.wait_ge(s_ready, BLOCKS)
                pe.wait_ge(hT_copied, BLOCKS)
                s_cols = s_all[:, :, :].rearrange("p h b -> p (h b)")
                for half in range(2):
                    pe.transpose(psT[0][:, half * P:(half + 1) * P], s_cols[:, half * P:(half + 1) * P],
                                 ident[:, :]).then_inc(sT_ready, 1)

        @block.gpsimd
        def _(pool):
            def step(at):
                a, z = at(1), at(2)
                if a and query:
                    for part, (ready, kept) in enumerate(((hT_high, "hT_hi"), (hT_low, "hT_lo"))):
                        pool.wait_ge(ready, a.number + 1)
                        pool.tensor_copy(res[kept][:, :, a.number, :],
                                         hT[:, a.parity, part, :].rearrange("p (t q) -> p t q", t=DT)
                                         ).then_inc(hT_kept, 1)
                if z and query:
                    pool.wait_ge(gT_low, z.number + 1)
                    pool.wait_ge(gT_high, z.number + 1)
                    hold(pool, held_store)
                    pool.dma_start(res["g_dram"][z.number], gT[:, z.parity, :, :]).then_inc(stored[z.parity], 16)
                if z and not query:
                    n = z.number
                    if isinstance(n, int) and n == 0:
                        pool.wait_ge(w_loaded, 48)
                    pool.wait_ge(feats_copied, n + 1)
                    ge(pool, record_ready, n)
                    pool.tensor_tensor(prod[:, 1, :].rearrange("p (g f) -> p g f", g=GROUPS),
                                       fx[:, z.parity, :, 0:GH * F],
                                       asn[:, 1, :].rearrange("p (g f) -> p g f", g=GROUPS),
                                       ALU.mult).then_inc(neigh_prod_ready, 1)
                    pool.wait_ge(record_ready, n + 1)
                    hold(pool, held_store)
                    pool.dma_start(res["fx_dram"][z.number], fx[:, z.parity, :, :]).then_inc(stored[z.parity], 16)

            pipeline(pool, step, 2)
            if query:
                pool.wait_ge(hT_kept, 2 * BLOCKS)
                pool.wait_ge(v_low, BLOCKS)
            for s in stored:
                pool.wait_ge(s, 16 * BLOCKS // 2)

        @block.vector
        def _(dve):
            SMALL = 6

            def variance(b):
                n = b.number
                dve.wait_ge(x_loaded[b.parity], 16 * (b.pair + 1))
                dve.bn_stats(stats[:, :], xin[:, b.parity, :]).then_inc(dve_stat, 1)
                dve.wait_ge(dve_stat, SMALL * n + 1)
                hold(dve, held)
                dve.bn_aggr(mv[:, :], stats[:, :]).then_inc(dve_stat, 1)
                dve.wait_ge(dve_stat, SMALL * n + 2)
                dve.tensor_scalar(var[:, :], mv[:, 1:2], LN_EPS, None, ALU.add).then_inc(var_ready, 1)

            def norm(b):
                n = b.number
                dve.wait_ge(std_ready, n + 1)
                dve.reciprocal(r0[:, :], std[:, :]).then_inc(dve_stat, 1)
                dve.wait_ge(dve_stat, SMALL * n + 3)
                dve.scalar_tensor_tensor(out=vrr[:, :], in0=r0[:, :], scalar=var[:, :], in1=r0[:, :],
                                         op0=ALU.mult, op1=ALU.mult).then_inc(dve_stat, 1)
                dve.wait_ge(dve_stat, SMALL * n + 4)
                dve.tensor_scalar(corr[:, :], vrr[:, :], -0.5, 1.5, ALU.mult, ALU.add).then_inc(dve_stat, 1)
                dve.wait_ge(dve_stat, SMALL * n + 5)
                dve.tensor_tensor(rstd[:, b.parity:b.parity + 1], r0[:, :], corr[:, :], ALU.mult).then_inc(dve_stat, 1)
                dve.wait_ge(dve_stat, SMALL * n + 6)
                dve.scalar_tensor_tensor(out=shift[:, b.parity:b.parity + 1], in0=mv[:, 0:1], scalar=-1.0,
                                         in1=rstd[:, b.parity:b.parity + 1],
                                         op0=ALU.mult, op1=ALU.mult).then_inc(norm_ready, 1)

            def scale_g(z):
                n = z.number
                dve.wait_ge(y_ready, n + 1)
                ge(dve, gs_ready, n)
                dve.tensor_reduce(gtop[:, :], psY[z.parity][:, :], AX.X, ALU.max,
                                  apply_absolute_value=True).then_inc(g_step, 1)
                dve.wait_ge(g_step, 3 * n + 1)
                dve.tensor_scalar(gunit[:, :], gtop[:, :], LEAST, 1.0 / G_TOP, ALU.max, ALU.mult).then_inc(g_step, 1)
                dve.wait_ge(g_step, 3 * n + 2)
                dve.tensor_tensor(res["row_scale"][:, bass.ds(n, 1)], gunit[:, :], res["m_unit"][:, :], ALU.mult)\
                   .then_inc(res["row_scale_ready"], 1)
                dve.reciprocal(ginv[:, :], gunit[:, :]).then_inc(g_step, 1)
                dve.wait_ge(g_step, 3 * n + 3)
                ge(dve, gT_ready, n)
                dve.tensor_scalar(gs[:, :], psY[z.parity][:, :], ginv[:, :], None, ALU.mult).then_inc(gs_ready, 1)

            def split_hT(a):
                dve.wait_ge(hT_high, a.number + 1)
                dve.tensor_tensor(hT[:, a.parity, 1, :], psT[a.parity][:, :], hT[:, a.parity, 0, :],
                                  ALU.subtract).then_inc(hT_low, 1)

            def split_v(z):
                dve.wait_ge(v_high, z.number + 1)
                dve.tensor_tensor(res["v_lo"][:, z.number, :], psV[z.parity][:, :], res["v_hi"][:, z.number, :],
                                  ALU.subtract).then_inc(v_low, 1)

            def split_g(z):
                dve.wait_ge(gT_high, z.number + 1)
                dve.tensor_tensor(gT[:, z.parity, 1, :], psG[:, :], gT[:, z.parity, 0, :],
                                  ALU.subtract).then_inc(gT_low, 1)

            def attention_terms(z):
                n = z.number
                if isinstance(n, int) and n == 0:
                    dve.wait_ge(w_loaded, 48)
                dve.wait_ge(feats_copied, n + 1)
                ge(dve, s_ready, n)
                dve.tensor_tensor(prod[:, 0, :].rearrange("p (g f) -> p g f", g=GROUPS),
                                  fx[:, z.parity, :, 0:GH * F], asn[:, 0, :].rearrange("p (g f) -> p g f", g=GROUPS),
                                  ALU.mult).then_inc(self_prod_ready, 1)
                dve.wait_ge(self_prod_ready, n + 1)
                dve.tensor_reduce(s_all[:, :, n], prod[:, 0, :].rearrange("p (h f) -> p h f", h=HEADS),
                                  AX.X, ALU.add).then_inc(s_ready, 1)
                dve.wait_ge(neigh_prod_ready, n + 1)
                dve.tensor_reduce(fx[:, z.parity, :, GH * F:FX],
                                  prod[:, 1, :].rearrange("p (g h f) -> p g h f", g=GROUPS, h=GH),
                                  AX.X, ALU.add, negate=True).then_inc(record_ready, 1)

            def step(at):
                b, a, z = at(0), at(1), at(2)
                if b:
                    variance(b)
                if z and query:
                    scale_g(z)
                if a and query:
                    split_hT(a)
                if b:
                    norm(b)
                if z and not query:
                    attention_terms(z)
                if z and query:
                    split_v(z)
                    split_g(z)

            pipeline(dve, step, 2)


def attend(nc, ident, res):
    with ExitStack() as stack:
        sb, ps, sem = open_allocator(nc, stack, "a_")
        adj = sb("adj", [P, N])
        scores = sb("scores", [P, N])
        pT_hi = sb("pT_hi", [P, N], F16)
        pT_lo = sb("pT_lo", [P, N], F16)
        gT = sb("gT", [P, 2, 2, D], F16)
        row_scale = sb("row_scale", [P, 2])
        maxes = sb("maxes", [P, CHUNKS])
        neg_max = sb("neg_max", [P, 2])
        sums = sb("sums", [P, 2])
        recip = sb("recip", [P, 1])
        mean = sb("mean", [P, D])
        x_in = sb("x_in", [P, D])
        x1_out = sb("x1_out", [P, D])
        psS = [ps("psS0"), ps("psS1")]
        psT = [ps("psT0"), ps("psT1")]
        psU = [ps("psU0"), ps("psU1")]
        x_loaded, x1_stored = sem("x_loaded"), sem("x1_stored")
        adj_loaded = [sem(f"adj_loaded{q}") for q in range(CHUNKS // 2)]
        g_loaded = [sem("g_loaded0"), sem("g_loaded1")]
        scale_ready = sem("scale_ready")
        scores_ready, scores_taken = sem("scores_ready"), sem("scores_taken")
        neg_ready, exp_ready = sem("neg_ready"), sem("exp_ready")
        pT_ready, pT_high, pT_low = sem("pT_ready"), sem("pT_high"), sem("pT_low")
        u_ready, recip_ready, mean_ready = sem("u_ready"), sem("recip_ready"), sem("mean_ready")
        x1_ready = sem("x1_ready")
        held, held_store = sem("held"), sem("held_store")
        block = stack.enter_context(nc.Block())
        adj_rows = res["adj"].rearrange("(b p) m -> b p m", p=P)
        x_rows = res["x"].rearrange("(b p) d -> b p d", p=P)
        x1_rows = res["x1_dram"].rearrange("(b p) d -> b p d", p=P)

        @block.sync
        def _(sp):
            def step(at):
                b = at(0)
                ge(sp, scores_ready, CHUNKS * (b.number - 1))
                sp.dma_start(gT[:, b.parity, :, :], res["g_dram"][b.number]).then_inc(g_loaded[b.parity], 16)
                for q in range(CHUNKS // 2):
                    ge(sp, scores_taken, CHUNKS * (b.number - 1) + 2 * q + 2)
                    cols = slice(2 * q * CHUNK, (2 * q + 2) * CHUNK)
                    sp.dma_start(adj[:, cols], adj_rows[b.number, :, cols]).then_inc(adj_loaded[q], 16)

            pipeline(sp, step, 0)

        @block.gpsimd
        def _(pool):
            def step(at):
                a = at(1)
                if a:
                    ge(pool, x1_ready, a.number)
                    hold(pool, held_store)
                    pool.dma_start(x_in[:, :], x_rows[a.number]).then_inc(x_loaded, 16)
                    pool.wait_ge(x1_ready, a.number + 1)
                    hold(pool, held_store)
                    pool.dma_start(x1_rows[a.number], x1_out[:, :]).then_inc(x1_stored, 16)

            pipeline(pool, step, 1)
            pool.wait_ge(x1_stored, 16 * BLOCKS)

        @block.tensor
        def _(pe):
            def transpose_p(a, c):
                if c == 0:
                    pe.wait_ge(exp_ready, a.number + 1)
                ge(pe, pT_low, CHUNKS * a.number + c - 1)
                for t in range(TPC):
                    col = c * CHUNK + t * P
                    mm = pe.transpose(psT[c % 2][:, t * P:(t + 1) * P], scores[:, col:col + P], ident[:, :])
                mm.then_inc(pT_ready, 1)

            def score(b, c):
                if c == 0:
                    pe.wait_ge(g_loaded[b.parity], 16 * (b.pair + 1))
                ge(pe, scores_taken, CHUNKS * b.number + c - 1)
                parts = [(g, t, hT) for t in range(DT) for g, hT in ((1, "hT_hi"), (0, "hT_lo"), (0, "hT_hi"))]
                for i, (g, t, hT) in enumerate(parts):
                    mm = pe.matmul(psS[c % 2][:, :], gT[:, b.parity, g, t * P:(t + 1) * P],
                                   res[hT][:, t, c * TPC:(c + 1) * TPC, :],
                                   start=(i == 0), stop=(i == len(parts) - 1))
                mm.then_inc(scores_ready, 1)

            def weighted_mean(a):
                ge(pe, mean_ready, a.number - 1)
                for k in range(BLOCKS):
                    if k % TPC == 0:
                        pe.wait_ge(pT_low, CHUNKS * a.number + k // TPC + 1)
                    for i, (pT, v) in enumerate(((pT_lo, "v_hi"), (pT_hi, "v_lo"), (pT_hi, "v_hi"))):
                        mm = pe.matmul(psU[a.parity][:, :], pT[:, k * P:(k + 1) * P], res[v][:, k, :],
                                       start=(k == 0 and i == 0), stop=(k == BLOCKS - 1 and i == 2))
                mm.then_inc(u_ready, 1)

            def step(at):
                b, a = at(0), at(1)
                for c in range(CHUNKS):
                    if a:
                        transpose_p(a, c)
                    if b:
                        score(b, c)
                if a:
                    weighted_mean(a)

            pipeline(pe, step, 1)

        @block.scalar
        def _(act):
            def step(at):
                b, a = at(0), at(1)
                for c in range(CHUNKS):
                    if a:
                        act.wait_ge(pT_ready, CHUNKS * a.number + c + 1)
                        act.activation(pT_hi[:, c * CHUNK:(c + 1) * CHUNK], psT[c % 2][:, :], ACT.Copy,
                                       scale=P_SCALE).then_inc(pT_high, 1)
                if b:
                    act.wait_ge(neg_ready, b.number + 1)
                    act.activation(scores[:, :], scores[:, :], ACT.Exp, bias=neg_max[:, b.parity:b.parity + 1],
                                   accum_out=sums[:, b.parity:b.parity + 1]).then_inc(exp_ready, 1)

            pipeline(act, step, 1)

        @block.vector
        def _(dve):
            def step(at):
                b, a = at(0), at(1)
                if b:
                    ge(dve, scores_taken, CHUNKS * (b.number - 1))
                    dve.tensor_copy(row_scale[:, b.parity:b.parity + 1], res["row_scale"][:, bass.ds(b.number, 1)]
                                    ).then_inc(scale_ready, 1)
                    dve.wait_ge(scale_ready, b.number + 1)
                for c in range(CHUNKS):
                    cols = slice(c * CHUNK, (c + 1) * CHUNK)
                    if a:
                        dve.wait_ge(pT_high, CHUNKS * a.number + c + 1)
                        dve.scalar_tensor_tensor(out=pT_lo[:, cols], in0=psT[c % 2][:, :], scalar=P_SCALE,
                                                 in1=pT_hi[:, cols], op0=ALU.mult, op1=ALU.subtract
                                                 ).then_inc(pT_low, 1)
                    if b:
                        dve.wait_ge(adj_loaded[c // 2], 16 * (b.number + 1))
                        if c == 0:
                            ge(dve, neg_ready, b.number)
                        dve.wait_ge(scores_ready, CHUNKS * b.number + c + 1)
                        hold(dve, held)
                        dve.tensor_tensor_reduce(out=scores[:, cols], in0=psS[c % 2][:, :], in1=adj[:, cols],
                                                 scale=row_scale[:, b.parity:b.parity + 1], scalar=-3.0e38,
                                                 op0=ALU.mult, op1=ALU.max, accum_out=maxes[:, c:c + 1]
                                                 ).then_inc(scores_taken, 1)
                if b:
                    dve.wait_ge(scores_taken, CHUNKS * (b.number + 1))
                    dve.tensor_reduce(neg_max[:, b.parity:b.parity + 1], maxes[:, :], AX.X, ALU.max,
                                      negate=True).then_inc(neg_ready, 1)
                if a:
                    dve.wait_ge(exp_ready, a.number + 1)
                    dve.reciprocal(recip[:, :], sums[:, a.parity:a.parity + 1]).then_inc(recip_ready, 1)
                    dve.wait_ge(recip_ready, a.number + 1)
                    dve.wait_ge(u_ready, a.number + 1)
                    ge(dve, x1_ready, a.number)
                    dve.scalar_tensor_tensor(out=mean[:, :], in0=psU[a.parity][:, :], scalar=recip[:, :],
                                             in1=res["v_unit"][:, :], op0=ALU.mult, op1=ALU.mult
                                             ).then_inc(mean_ready, 1)
                    dve.wait_ge(mean_ready, a.number + 1)
                    dve.wait_ge(x_loaded, 16 * (a.number + 1))
                    ge(dve, x1_stored, 16 * a.number)
                    dve.tensor_tensor(x1_out[:, :], mean[:, :], x_in[:, :], ALU.add).then_inc(x1_ready, 1)

            pipeline(dve, step, 1)


def aggregate(nc, ident, res):
    KS = 8
    AS = 4
    MT = MC // P
    HALVES = MC // CHUNK
    PAIRS = GH // 2
    ACT_HEADS = 2
    VEC_HEADS = GH - ACT_HEADS
    LEAD = 2
    FAR = 1e19
    with ExitStack() as stack:
        sb, ps, sem = open_allocator(nc, stack, "w_")
        far = sb("far", [P, AS, MC])
        fx = sb("fx", [P, KS, FX])
        s_rows = sb("s_rows", [P, 2, GH, MC])
        w = sb("w", [P, KS, GH, MC])
        zeros = sb("zeros", [P, P], F16)
        ones = sb("ones", [P, 32])
        bias = sb("bias", [P, HEADS * F])
        outT = sb("outT", [P, PAIRS + 1, MC])
        y = sb("y", [P, MT, GH * F])
        x1 = outT[:, 0:PAIRS, :].rearrange("p a m -> p (a m)").rearrange("p (t d) -> p t d", t=MT)
        recip = sb("recip", [P, MT, GH])
        psO = [[ps(f"psO{p}{half}") for half in range(HALVES)] for p in range(PAIRS)]
        psR = [ps(f"psR{half}") for half in range(HALVES)]
        psN = [ps("psN0"), ps("psN1")]
        adj_loaded = [sem(f"adj_loaded{i}") for i in range(AS)]
        fx_loaded = [sem(f"fx_loaded{i}") for i in range(KS)]
        s_loaded, bias_loaded, x1_loaded = sem("s_loaded"), sem("bias_loaded"), sem("x1_loaded")
        const_ready = sem("const_ready")
        far_ready, diff_ready = sem("far_ready"), sem("diff_ready")
        squared, pool_squared, exped, masked = sem("squared"), sem("pool_squared"), sem("exped"), sem("masked")
        w_used = sem("w_used")
        outT_copied, nat_ready, nat_taken = sem("outT_copied"), sem("nat_ready"), sem("nat_taken")
        eps_added, recip_ready, biased, y_ready = sem("eps_added"), sem("recip_ready"), sem("biased"), sem("y_ready")
        y_stored, held = sem("y_stored"), sem("held")
        block = stack.enter_context(nc.Block())
        adjT_view = res["adjT"].rearrange("(b p) (c m) -> b c p m", p=P, m=MC)
        s_view = res["s_dram"].rearrange("(g h b) m -> g h (b m)", g=GROUPS, h=GH)
        x1_view = res["x1_dram"].rearrange("(c t p) (g d) -> c g p t d", t=MT, p=P, g=GROUPS)
        y_view = res["out"].rearrange("(c t p) (g d) -> c g p t d", t=MT, p=P, g=GROUPS)

        BANKS = (PAIRS + 1) * HALVES
        PARTS = GROUPS * (N // MC)
        TURNS = BLOCKS // KS

        PIECE = 2
        PIECES = MT // PIECE
        ADD_AT = KS - PIECES - 1
        LOAD_AT = 3

        def nothing(*_):
            pass

        def sweep(eng, step, turn_tile=nothing, tile=nothing, first=nothing, late=nothing, last=nothing):
            def turn_of(o, c, group, turn, before=nothing, behind=nothing):
                for slot in range(KS):
                    u = TURNS * o + turn
                    before(slot)
                    step(o, c, group, KS * turn + slot, slot, u, KS * u + slot)
                    behind(slot)

            def part(c, group):
                o = GROUPS * c + group
                first(o, c, group)
                turn_of(o, c, group, 0)
                with eng.Fori(1, TURNS - 2) as turn:
                    turn_of(o, c, group, turn)
                if isinstance(o, int) and o == 0:
                    turn_of(o, c, group, TURNS - 2)
                    turn_of(o, c, group, TURNS - 1)
                else:
                    turn_of(o, c, group, TURNS - 2, lambda t: turn_tile(o - 1, t), lambda t: tile(o - 1, t))
                    turn_of(o, c, group, TURNS - 1, behind=lambda slot: late(o - 1, c - 1 + group, 1 - group, slot))
                    last(o - 1, c - 1 + group, 1 - group)

            part(0, 0)
            with eng.Fori(0, N // MC - 1) as c:
                part(c, 1)
                part(c + 1, 0)
            part(N // MC - 1, 1)

        @block.sync
        def _(sp):
            sp.dma_start(bias[:, :], res["biases"].partition_broadcast(P)).then_inc(bias_loaded, 16)

            def load_x1(q, c, group, slot=LOAD_AT):
                if slot != LOAD_AT:
                    return
                sp.wait_ge(nat_ready, MT * (q + 1))
                sp.dma_start(x1[:, :, :], x1_view[c, group]).then_inc(x1_loaded, 16)

            def first(o, c, group):
                if not (isinstance(o, int) and o < 2):
                    sp.wait_ge(w_used, KS + BLOCKS * (o - 1))
                sp.dma_start(s_rows[:, group, :, :],
                             s_view[group, :, bass.ds(c * MC, MC)].partition_broadcast(P)).then_inc(s_loaded, 16)

            def step(o, c, group, k, slot, u, g):
                sp.wait_ge(masked, g + 1)
                hold(sp, held)
                sp.dma_start(far[:, slot % AS, :], adjT_view[k, c]).then_inc(adj_loaded[slot % AS], 16)
                sp.wait_ge(w_used, g + 1)
                sp.dma_start(fx[:, slot, :], res["fx_dram"][k, :, group, :]).then_inc(fx_loaded[slot], 16)

            sweep(sp, step, first=first, late=load_x1)
            load_x1(PARTS - 1, N // MC - 1, 1)

        @block.scalar
        def _(act):
            def square(o, group, slot, u, g):
                act.wait_ge(s_loaded, 16 * (o + 1))
                act.wait_ge(fx_loaded[slot], 16 * (u + 1))
                act.wait_ge(w_used, g + 1)
                for a in range(ACT_HEADS):
                    act.activation(w[:, slot, a, :], s_rows[:, group, a, :], ACT.Square,
                                   bias=fx[:, slot, GH * F + a:GH * F + a + 1]).then_inc(squared, 1)

            def step(o, c, group, k, slot, u, g):
                ahead = (slot + 1) % KS, u + (slot + 1) // KS, g + 1
                if not (isinstance(k, int) and k + 1 >= BLOCKS):
                    square(o, group, *ahead)
                elif not (isinstance(o, int) and o == PARTS - 1):
                    square(o + 1, 1 - group, *ahead)
                act.wait_ge(squared, ACT_HEADS * (g + 1))
                act.wait_ge(pool_squared, g + 1)
                act.activation(w[:, slot, :, :], w[:, slot, :, :], ACT.Exp, scale=-1.0).then_inc(exped, 1)

            def first(o, c, group):
                if isinstance(o, int) and o == 0:
                    square(o, group, 0, 0, 0)

            def store_y(q, c, group):
                act.wait_ge(y_ready, 1 + PIECES * (q + 1))
                act.dma_start(y_view[c, group], y[:, :, :]).then_inc(y_stored, 16)

            sweep(act, step, first=first, last=store_y)
            store_y(PARTS - 1, N // MC - 1, 1)
            act.wait_ge(y_stored, 16 * (PARTS + 1))

        @block.gpsimd
        def _(pool):
            pool.sem_inc(w_used, KS)
            pool.sem_inc(masked, AS)
            pool.sem_inc(nat_taken, 2)
            pool.sem_inc(y_stored, 16)
            pool.sem_inc(y_ready, 1)
            pool.memset(zeros[:, :], 0.0).then_inc(const_ready, 1)
            pool.memset(ones[:, :], 1.0).then_inc(const_ready, 1)

            def step(o, c, group, k, slot, u, g):
                pool.wait_ge(diff_ready, VEC_HEADS * (g + 1))
                half = w[:, slot, ACT_HEADS:GH, :]
                pool.tensor_tensor(half, half, half, ALU.mult).then_inc(pool_squared, 1)

            def add_bias(q, c, group, slot):
                if slot >= PIECES:
                    return
                n = PIECES * q + slot + 1
                pool.wait_ge(nat_taken, 2 + PIECE * n)
                columns = bias[:, group * GH * F:(group + 1) * GH * F]
                piece = y[:, PIECE * slot:PIECE * (slot + 1), :]
                pool.tensor_tensor(piece, piece, columns.unsqueeze(1).broadcast_to([P, PIECE, GH * F]),
                                   ALU.add).then_inc(biased, 1)

            pool.wait_ge(bias_loaded, 16)
            sweep(pool, step, late=add_bias)
            for slot in range(PIECES):
                add_bias(PARTS - 1, N // MC - 1, 1, slot)

        @block.vector
        def _(dve):
            def differ(o, group, slot, u, g):
                dve.wait_ge(s_loaded, 16 * (o + 1))
                dve.wait_ge(adj_loaded[slot % AS], 16 * (KS // AS * u + slot // AS + 1))
                here = far[:, slot % AS, :]
                dve.tensor_scalar(here, here, 0.0, FAR, ALU.is_le, ALU.mult).then_inc(far_ready, 1)
                dve.wait_ge(fx_loaded[slot], 16 * (u + 1))
                dve.wait_ge(w_used, g + 1)
                dve.wait_ge(far_ready, g + 1)
                for a in range(ACT_HEADS, GH):
                    dve.scalar_tensor_tensor(out=w[:, slot, a, :], in0=s_rows[:, group, a, :],
                                             scalar=fx[:, slot, GH * F + a:GH * F + a + 1], in1=here,
                                             op0=ALU.add, op1=ALU.add).then_inc(diff_ready, 1)

            def mask(slot, g):
                dve.wait_ge(exped, g + 1)
                dve.scalar_tensor_tensor(out=w[:, slot, 0:ACT_HEADS, :],
                                         in0=far[:, slot % AS, :].unsqueeze(1).broadcast_to([P, ACT_HEADS, MC]),
                                         scalar=0.0, in1=w[:, slot, 0:ACT_HEADS, :],
                                         op0=ALU.is_equal, op1=ALU.mult).then_inc(masked, 1)

            def step(o, c, group, k, slot, u, g):
                ahead = (slot + LEAD) % KS, u + (slot + LEAD) // KS, g + LEAD
                if not (isinstance(k, int) and k + LEAD >= BLOCKS):
                    differ(o, group, *ahead)
                elif not (isinstance(o, int) and o == PARTS - 1):
                    differ(o + 1, 1 - group, *ahead)
                if isinstance(k, int) and k == 0 and not (isinstance(o, int) and o == 0):
                    copy_out(o - 1)
                mask(slot, g)

            def copy_out(q):
                dve.wait_ge(w_used, KS + BLOCKS * (q + 1))
                dve.wait_ge(y_ready, 1 + PIECES * q)
                for i, banks in enumerate(psO + [psR]):
                    for half in range(HALVES):
                        dve.tensor_copy(outT[:, i, half * CHUNK:(half + 1) * CHUNK], banks[half][:, :]
                                        ).then_inc(outT_copied, 1)

            def add_eps(q, t):
                dve.wait_ge(nat_ready, MT * q + t + 1)
                sums = psN[t % 2][:, PAIRS * P:(PAIRS + 1) * P].rearrange("p (a r) -> p a r", a=GH)[:, :, 0]
                dve.tensor_scalar(recip[:, t, :], sums, SUM_EPS, None, ALU.add).then_inc(eps_added, 1)

            def invert(q, t):
                dve.wait_ge(eps_added, MT * q + t + 1)
                dve.reciprocal(recip[:, t, :], recip[:, t, :]).then_inc(recip_ready, 1)

            def divide(q, t):
                if t == 0:
                    dve.wait_ge(y_stored, 16 * (q + 1))
                dve.wait_ge(recip_ready, MT * q + t + 1)
                dve.tensor_tensor(y[:, t, :].rearrange("p (a f) -> p a f", a=GH),
                                  psN[t % 2][:, 0:PAIRS * P].rearrange("p (a f) -> p a f", a=GH),
                                  recip[:, t, :].unsqueeze(2).broadcast_to([P, GH, F]), ALU.mult
                                  ).then_inc(nat_taken, 1)

            def before_step(q, t):
                if t > 0:
                    invert(q, t - 1)

            def behind_step(q, t):
                if t > 0:
                    divide(q, t - 1)
                add_eps(q, t)

            def finish(q, c, group, slot):
                if slot == 0:
                    invert(q, MT - 1)
                if slot == 1:
                    divide(q, MT - 1)
                add_x1(q, c, group, slot)

            def add_x1(q, c, group, slot):
                i = slot - ADD_AT
                if not 0 <= i < PIECES:
                    return
                if i == 0:
                    dve.wait_ge(x1_loaded, 16 * (q + 1))
                n = PIECES * q + i + 1
                dve.wait_ge(biased, n)
                piece = y[:, PIECE * i:PIECE * (i + 1), :]
                dve.scalar_tensor_tensor(out=piece, in0=piece, scalar=0.0, in1=x1[:, PIECE * i:PIECE * (i + 1), :],
                                         op0=ALU.max, op1=ALU.add).then_inc(y_ready, 1)

            def first(o, c, group):
                if isinstance(o, int) and o == 0:
                    for slot in range(LEAD):
                        differ(o, group, slot, 0, slot)

            sweep(dve, step, turn_tile=before_step, tile=behind_step, first=first, late=finish)
            copy_out(PARTS - 1)
            for t in range(MT):
                add_eps(PARTS - 1, t)
                invert(PARTS - 1, t)
                divide(PARTS - 1, t)
            for i in range(PIECES):
                add_x1(PARTS - 1, N // MC - 1, 1, ADD_AT + i)

        @block.tensor
        def _(pe):
            pe.wait_ge(const_ready, 2)

            def first(o, c, group):
                ge(pe, outT_copied, BANKS * o)
                for bank in psO[0] + psO[1] + psR:
                    pe.matmul(bank[:, :].rearrange("p (i q) -> p i q", q=P), zeros[:, :],
                              zeros[:, :].unsqueeze(1).broadcast_to([P, CHUNK // P, P]), start=True, stop=False,
                              skip_group_check=True)

            def step(o, c, group, k, slot, u, g):
                for pair in reversed(range(PAIRS)):
                    if pair:
                        pe.wait_ge(exped, g + 1)
                    else:
                        pe.wait_ge(masked, AS + g + 1)
                    for half in range(HALVES):
                        for i in range(2):
                            a = 2 * pair + i
                            pe.matmul(psO[pair][half][F * i:F * i + F, :], fx[:, slot, F * a:F * a + F],
                                      w[:, slot, a, half * CHUNK:(half + 1) * CHUNK],
                                      start=False, stop=False, skip_group_check=True)
                for half in range(HALVES):
                    for a in range(GH):
                        mm = pe.matmul(psR[half][32 * a:32 * a + 32, :], ones[:, :],
                                       w[:, slot, a, half * CHUNK:(half + 1) * CHUNK],
                                       start=False, stop=False, skip_group_check=True)
                mm.then_inc(w_used, 1)

            def turn_back(q, t):
                if t == 0:
                    pe.wait_ge(outT_copied, BANKS * (q + 1))
                pe.wait_ge(nat_taken, MT * q + t + 1)
                for i in range(PAIRS + 1):
                    mm = pe.transpose(psN[t % 2][:, i * P:(i + 1) * P], outT[:, i, t * P:(t + 1) * P], ident[:, :])
                mm.then_inc(nat_ready, 1)

            sweep(pe, step, turn_tile=turn_back, first=first)
            for t in range(MT):
                turn_back(PARTS - 1, t)


def program(nc, x, adj, adjT, wqT, wkT, wv, wvT, wk1, attn_self, attn_neigh, biases, out):
    g_dram = nc.dram_tensor("g_dram", [BLOCKS, P, 2, D], F16).ap()
    x1_dram = nc.dram_tensor("x1_dram", [N, D], F32).ap()
    fx_dram = nc.dram_tensor("fx_dram", [BLOCKS, P, GROUPS, FX], F32).ap()
    s_dram = nc.dram_tensor("s_dram", [HEADS * BLOCKS, P], F32).ap()
    with nc.sbuf_tensor("ident", [P, P], F32) as ident:
        make_identity(nc, ident)
        with ExitStack() as stack:
            def resident(name, shape, dt):
                return stack.enter_context(nc.sbuf_tensor(name, shape, dt))

            res = {"x": x, "adj": adj, "g_dram": g_dram, "x1_dram": x1_dram,
                   "v_hi": resident("v_hi", [P, BLOCKS, D], F16), "v_lo": resident("v_lo", [P, BLOCKS, D], F16),
                   "v_unit": resident("v_unit", [P, D], F32),
                   "hT_hi": resident("hT_hi", [P, DT, BLOCKS, P], F16),
                   "hT_lo": resident("hT_lo", [P, DT, BLOCKS, P], F16),
                   "row_scale": resident("row_scales", [P, BLOCKS], F32)}
            with nc.sbuf_tensor("m_parts", [P, 2, DT, D], F16) as m_parts, \
                    nc.sbuf_tensor("v_parts", [P, 2, DT, D], F16) as v_parts, \
                    nc.sbuf_tensor("score_unit", [P, 1], F32) as m_unit, nc.semaphore("row_scale_ready") as ready:
                prepare_weights(nc, ident, wqT, wkT, wv, wvT, m_parts, v_parts, m_unit, res["v_unit"])
                project_rows(nc, QUERY, ident, x, m_parts,
                             res | {"v_parts": v_parts, "m_unit": m_unit, "row_scale_ready": ready})
            attend(nc, ident, res)
        with nc.sbuf_tensor("wk1_sb", [P, DT, D], F32) as wk1_sb:
            project_rows(nc, GRAPH, ident, x1_dram, wk1_sb[:, :, :],
                         {"w_dram": wk1, "attn_self": attn_self, "attn_neigh": attn_neigh,
                          "fx_dram": fx_dram, "s_dram": s_dram})
        aggregate(nc, ident, {"adjT": adjT, "fx_dram": fx_dram, "s_dram": s_dram, "x1_dram": x1_dram,
                              "biases": biases, "out": out})


def kernel(x, adj, L0_gnn_W_Q, L0_gnn_W_K, L0_gnn_W_V, L1_gnn_kernels, L1_gnn_attn_self, L1_gnn_attn_neigh,
           L1_gnn_biases):
    import concourse.bacc as bacc
    from concourse.bass_utils import run_bass_kernel_spmd

    def laid(a):
        return np.ascontiguousarray(np.asarray(a))

    arrays = {
        "x": laid(x), "adj": laid(adj), "adjT": laid(np.asarray(adj).T),
        "wqT": laid(np.asarray(L0_gnn_W_Q).T), "wkT": laid(np.asarray(L0_gnn_W_K).T),
        "wv": laid(L0_gnn_W_V), "wvT": laid(np.asarray(L0_gnn_W_V).T),
        "wk1": laid(np.asarray(L1_gnn_kernels).transpose(1, 0, 2).reshape(D, HEADS * F)),
        "attn_self": laid(L1_gnn_attn_self).reshape(-1), "attn_neigh": laid(L1_gnn_attn_neigh).reshape(-1),
        "biases": laid(L1_gnn_biases).reshape(-1),
    }
    nc = bacc.Bacc("TRN2", target_bir_lowering=False, num_devices=1)
    args = [nc.dram_tensor(name, a.shape, F32, kind="ExternalInput").ap() for name, a in arrays.items()]
    out = nc.dram_tensor("out", (N, D), F32, kind="ExternalOutput").ap()
    program(nc, *args, out)
    result = run_bass_kernel_spmd(nc, [arrays], core_ids=[0])
    return result.results[0]["out"]
```
